# Optimizing a Trainium2 kernel written in Bass

```python
import numpy as np
import jax
import jax.numpy as jnp

def _softmax(x, axis=-1):
    return jax.nn.softmax(x, axis=axis)

def _gelu(x):
    return jax.nn.gelu(x, approximate=True)

def _silu(x):
    return jax.nn.silu(x)

def _sigmoid(x):
    return jax.nn.sigmoid(x)

def _layernorm(x, axis=-1, eps=1e-05):
    m = jnp.mean(x, axis=axis, keepdims=True)
    v = jnp.var(x, axis=axis, keepdims=True)
    return (x - m) / jnp.sqrt(v + eps)

def _scatter_add(tgt, idx, src, axis=0):
    return tgt.at[idx].add(src)

def _segment_sum(src, seg, n):
    return jax.ops.segment_sum(src, seg, n)
kernel_name = 'mk_seq_postln_d2_jaxref_r8_09be43'

def setup_inputs(seed: int=0):
    np.random.seed(seed)
    _w = jnp.asarray

    def _L0_attn_setup():
        import jax, jax.numpy as jnp
        import numpy as np
        H, DK, DV = (16, 128, 128)
        EPS = 1e-06

        def _causal_dw_conv(x, w):
            K = w.shape[0]
            T = x.shape[1]
            xp = jnp.pad(x, ((0, 0), (K - 1, 0), (0, 0)))
            out = w[0] * xp[:, 0:T, :]
            for i in range(1, K):
                out = out + w[i] * xp[:, i:i + T, :]
            return out

        def _rmsnorm(h, w):
            hf = h.astype(jnp.float32)
            var = jnp.mean(hf * hf, axis=-1, keepdims=True)
            return (hf * jax.lax.rsqrt(var + EPS)).astype(h.dtype) * w

        def _l2norm(x):
            return x * jax.lax.rsqrt(jnp.sum(x * x, axis=-1, keepdims=True) + EPS)
        key = jax.random.key(seed)
        ks = jax.random.split(key, 32)
        B, T, D = (1, 128, 256)
        LOW, I = (128, 1024)
        KD, VD = (H * DK, H * DV)
        s = 0.02
        f = jnp.float32
        return {'x': jax.random.normal(ks[0], (B, T, D), f), 'wq': jax.random.normal(ks[1], (D, KD), f) * s, 'wk': jax.random.normal(ks[2], (D, KD), f) * s, 'wv': jax.random.normal(ks[3], (D, VD), f) * s, 'conv_q': jax.random.normal(ks[4], (4, KD), f) * 0.2, 'conv_k': jax.random.normal(ks[5], (4, KD), f) * 0.2, 'conv_v': jax.random.normal(ks[6], (4, VD), f) * 0.2, 'wfa': jax.random.normal(ks[7], (D, LOW), f) * s, 'wfb': jax.random.normal(ks[8], (LOW, H), f) * s, 'wb': jax.random.normal(ks[9], (D, H), f) * s, 'wga': jax.random.normal(ks[10], (D, LOW), f) * s, 'wgb': jax.random.normal(ks[11], (LOW, VD), f) * s, 'a_log': jax.random.normal(ks[12], (H,), f) * 0.1, 'dt_bias': jnp.ones((H,), f), 'o_norm_w': jnp.ones((DV,), f), 'wo': jax.random.normal(ks[13], (VD, D), f) * s, 'ln1_w': jnp.ones((D,), f), 'ln2_w': jnp.ones((D,), f), 'w_gate': jax.random.normal(ks[14], (D, I), f) * s, 'w_up': jax.random.normal(ks[15], (D, I), f) * s, 'w_down': jax.random.normal(ks[16], (I, D), f) * s}
    _L0_attn_in = _L0_attn_setup()

    def _L0_ffn_setup():
        import jax, jax.numpy as jnp
        import numpy as np
        HIDDEN = 256
        INTER = 1024
        B, S = (4, 128)

        def _qmatmul(x, w_int8, scale):
            y = jnp.einsum('bsh,ho->bso', x, w_int8.astype(x.dtype))
            return y * scale
        key = jax.random.key(seed)
        ks = jax.random.split(key, 7)
        x = jax.random.normal(ks[0], (B, S, HIDDEN), dtype=jnp.float32)
        w_gate = jax.random.randint(ks[1], (HIDDEN, INTER), -128, 128, dtype=jnp.int32).astype(jnp.int8)
        w_up = jax.random.randint(ks[2], (HIDDEN, INTER), -128, 128, dtype=jnp.int32).astype(jnp.int8)
        w_down = jax.random.randint(ks[3], (INTER, HIDDEN), -128, 128, dtype=jnp.int32).astype(jnp.int8)
        s_gate = jax.random.uniform(ks[4], (INTER,), dtype=jnp.float32) * 0.02 + 0.001
        s_up = jax.random.uniform(ks[5], (INTER,), dtype=jnp.float32) * 0.02 + 0.001
        s_down = jax.random.uniform(ks[6], (HIDDEN,), dtype=jnp.float32) * 0.02 + 0.001
        return {'x': x, 'w_gate': w_gate, 'w_up': w_up, 'w_down': w_down, 's_gate': s_gate, 's_up': s_up, 's_down': s_down}
    _L0_ffn_in = _L0_ffn_setup()

    def _L1_attn_setup():
        import jax, jax.numpy as jnp
        import numpy as np
        B, T, HID = (1, 128, 256)
        H, DK, DV, M, KW = (16, 128, 128, 128, 4)
        SCALE = DK ** (-0.5)
        EPS = 1e-05

        def short_conv(x, w):
            K = w.shape[1]
            xp = jnp.pad(x, ((0, 0), (K - 1, 0), (0, 0)))
            t = x.shape[1]
            y = sum((xp[:, i:i + t] * w[:, i] for i in range(K)))
            return jax.nn.silu(y)

        def l2norm(x):
            return x * jax.lax.rsqrt(jnp.sum(x * x, axis=-1, keepdims=True) + 1e-06)

        def gsa2_scan(q, k, v, w, g, beta):
            b = q.shape[0]
            tm = lambda x: jnp.moveaxis(x, 1, 0)
            Sk0 = jnp.zeros((b, H, DK, M), q.dtype)
            Sv0 = jnp.zeros((b, H, M, DV), q.dtype)

            def step(carry, xs):
                Sk, Sv = carry
                q_t, k_t, v_t, w_t, g_t, b_t = xs
                gt = jnp.exp(g_t)
                bw = b_t[:, :, None] * w_t
                Sk = Sk * gt[:, :, None, :] + k_t[..., :, None] * bw[:, :, None, :]
                Sv = Sv * gt[..., None] + bw[..., None] * v_t[:, :, None, :]
                s = jnp.einsum('bhd,bhdm->bhm', q_t, Sk) * SCALE
                a = jax.nn.softmax(s, axis=-1)
                o_t = jnp.einsum('bhm,bhmd->bhd', a, Sv)
                return ((Sk, Sv), o_t)
            (_, _), o = jax.lax.scan(step, (Sk0, Sv0), (tm(q), tm(k), tm(v), tm(w), tm(g), tm(beta)))
            return jnp.moveaxis(o, 0, 1)
        key = jax.random.key(seed)
        ks = jax.random.split(key, 16)
        s = 0.02
        return {'hidden_states': jax.random.normal(ks[0], (B, T, HID), jnp.float32), 'Wq': jax.random.normal(ks[1], (HID, H * DK), jnp.float32) * s, 'Wk': jax.random.normal(ks[2], (HID, H * DK), jnp.float32) * s, 'Wv': jax.random.normal(ks[3], (HID, H * DV), jnp.float32) * s, 'Ww': jax.random.normal(ks[4], (HID, H * M), jnp.float32) * s, 'cq': jax.random.normal(ks[5], (H * DK, KW), jnp.float32) * 0.2, 'ck': jax.random.normal(ks[6], (H * DK, KW), jnp.float32) * 0.2, 'cv': jax.random.normal(ks[7], (H * DV, KW), jnp.float32) * 0.2, 'Wf1': jax.random.normal(ks[8], (HID, DV), jnp.float32) * s, 'Wf2': jax.random.normal(ks[9], (DV, H * M), jnp.float32) * s, 'Wb': jax.random.normal(ks[10], (HID, H), jnp.float32) * s, 'Wg1': jax.random.normal(ks[11], (HID, DV), jnp.float32) * s, 'Wg2': jax.random.normal(ks[12], (DV, H * DV), jnp.float32) * s, 'bg2': jnp.zeros((H * DV,), jnp.float32), 'norm_w': jnp.ones((DV,), jnp.float32), 'Wo': jax.random.normal(ks[13], (H * DV, HID), jnp.float32) * s}
    _L1_attn_in = _L1_attn_setup()

    def _L1_ffn_setup():
        import jax, jax.numpy as jnp
        import numpy as np
        D_MODEL, D_FF, NS, NR, KR = (256, 176, 2, 16, 4)
        B, S = (4, 256)

        def _moe_forward(u, shared_w1, shared_b1, shared_w2, shared_b2, routed_w1, routed_b1, routed_w2, routed_b2, centroids, bias):
            b, s, d = u.shape
            flat = u.reshape(-1, d)
            T = flat.shape[0]
            h = jax.nn.relu(jnp.einsum('td,ndf->ntf', flat, shared_w1) + shared_b1[:, None, :])
            shared_out = jnp.einsum('ntf,nfd->td', h, shared_w2) + shared_b2.sum(0)
            out = flat + shared_out
            scores = jax.nn.sigmoid(flat @ centroids.T) + bias
            vals, idx = jax.lax.top_k(scores, KR)
            gating = jnp.zeros_like(scores).at[jnp.arange(T)[:, None], idx].set(vals)
            gating = gating / jnp.clip(gating.sum(-1, keepdims=True), 1e-08)

            def step(acc, ew):
                w1, b1, w2, b2, g = ew
                hj = jax.nn.relu(flat @ w1 + b1)
                yj = hj @ w2 + b2
                return (acc + yj * g[:, None], None)
            rout0 = jnp.zeros_like(flat)
            rout, _ = jax.lax.scan(step, rout0, (routed_w1, routed_b1, routed_w2, routed_b2, gating.T))
            return (out + rout).reshape(b, s, d)
        key = jax.random.key(seed)
        ks = jax.random.split(key, 10)
        s1 = 1.0 / np.sqrt(D_MODEL)
        s2 = 1.0 / np.sqrt(D_FF)
        return {'u': jax.random.normal(ks[0], (B, S, D_MODEL), dtype=jnp.float32), 'shared_w1': jax.random.normal(ks[1], (NS, D_MODEL, D_FF), dtype=jnp.float32) * s1, 'shared_b1': jnp.zeros((NS, D_FF), dtype=jnp.float32), 'shared_w2': jax.random.normal(ks[2], (NS, D_FF, D_MODEL), dtype=jnp.float32) * s2, 'shared_b2': jnp.zeros((NS, D_MODEL), dtype=jnp.float32), 'routed_w1': jax.random.normal(ks[3], (NR, D_MODEL, D_FF), dtype=jnp.float32) * s1, 'routed_b1': jnp.zeros((NR, D_FF), dtype=jnp.float32), 'routed_w2': jax.random.normal(ks[4], (NR, D_FF, D_MODEL), dtype=jnp.float32) * s2, 'routed_b2': jnp.zeros((NR, D_MODEL), dtype=jnp.float32), 'centroids': jax.random.normal(ks[5], (NR, D_MODEL), dtype=jnp.float32) * s1, 'bias': jnp.zeros((NR,), dtype=jnp.float32)}
    _L1_ffn_in = _L1_ffn_setup()
    _d = {'L0_attn_x': _L0_attn_in['x'], 'L0_attn_wq': _L0_attn_in['wq'], 'L0_attn_wk': _L0_attn_in['wk'], 'L0_attn_wv': _L0_attn_in['wv'], 'L0_attn_conv_q': _L0_attn_in['conv_q'], 'L0_attn_conv_k': _L0_attn_in['conv_k'], 'L0_attn_conv_v': _L0_attn_in['conv_v'], 'L0_attn_wfa': _L0_attn_in['wfa'], 'L0_attn_wfb': _L0_attn_in['wfb'], 'L0_attn_wb': _L0_attn_in['wb'], 'L0_attn_wga': _L0_attn_in['wga'], 'L0_attn_wgb': _L0_attn_in['wgb'], 'L0_attn_a_log': _L0_attn_in['a_log'], 'L0_attn_dt_bias': _L0_attn_in['dt_bias'], 'L0_attn_o_norm_w': _L0_attn_in['o_norm_w'], 'L0_attn_wo': _L0_attn_in['wo'], 'L0_attn_ln1_w': _L0_attn_in['ln1_w'], 'L0_attn_ln2_w': _L0_attn_in['ln2_w'], 'L0_attn_w_gate': _L0_attn_in['w_gate'], 'L0_attn_w_up': _L0_attn_in['w_up'], 'L0_attn_w_down': _L0_attn_in['w_down'], 'L0_ffn_w_gate': _L0_ffn_in['w_gate'], 'L0_ffn_w_up': _L0_ffn_in['w_up'], 'L0_ffn_w_down': _L0_ffn_in['w_down'], 'L0_ffn_s_gate': _L0_ffn_in['s_gate'], 'L0_ffn_s_up': _L0_ffn_in['s_up'], 'L0_ffn_s_down': _L0_ffn_in['s_down'], 'L1_attn_Wq': _L1_attn_in['Wq'], 'L1_attn_Wk': _L1_attn_in['Wk'], 'L1_attn_Wv': _L1_attn_in['Wv'], 'L1_attn_Ww': _L1_attn_in['Ww'], 'L1_attn_cq': _L1_attn_in['cq'], 'L1_attn_ck': _L1_attn_in['ck'], 'L1_attn_cv': _L1_attn_in['cv'], 'L1_attn_Wf1': _L1_attn_in['Wf1'], 'L1_attn_Wf2': _L1_attn_in['Wf2'], 'L1_attn_Wb': _L1_attn_in['Wb'], 'L1_attn_Wg1': _L1_attn_in['Wg1'], 'L1_attn_Wg2': _L1_attn_in['Wg2'], 'L1_attn_bg2': _L1_attn_in['bg2'], 'L1_attn_norm_w': _L1_attn_in['norm_w'], 'L1_attn_Wo': _L1_attn_in['Wo'], 'L1_ffn_shared_w1': _L1_ffn_in['shared_w1'], 'L1_ffn_shared_b1': _L1_ffn_in['shared_b1'], 'L1_ffn_shared_w2': _L1_ffn_in['shared_w2'], 'L1_ffn_shared_b2': _L1_ffn_in['shared_b2'], 'L1_ffn_routed_w1': _L1_ffn_in['routed_w1'], 'L1_ffn_routed_b1': _L1_ffn_in['routed_b1'], 'L1_ffn_routed_w2': _L1_ffn_in['routed_w2'], 'L1_ffn_routed_b2': _L1_ffn_in['routed_b2'], 'L1_ffn_centroids': _L1_ffn_in['centroids'], 'L1_ffn_bias': _L1_ffn_in['bias']}
    _x0 = _d['L0_attn_x']
    _d['L0_attn_x'] = jax.random.normal(jax.random.fold_in(jax.random.key(seed), 1), (8, 256, 256), dtype=_x0.dtype)
    del _x0
    return _d

def reference(L0_attn_x, L0_attn_wq, L0_attn_wk, L0_attn_wv, L0_attn_conv_q, L0_attn_conv_k, L0_attn_conv_v, L0_attn_wfa, L0_attn_wfb, L0_attn_wb, L0_attn_wga, L0_attn_wgb, L0_attn_a_log, L0_attn_dt_bias, L0_attn_o_norm_w, L0_attn_wo, L0_attn_ln1_w, L0_attn_ln2_w, L0_attn_w_gate, L0_attn_w_up, L0_attn_w_down, L0_ffn_w_gate, L0_ffn_w_up, L0_ffn_w_down, L0_ffn_s_gate, L0_ffn_s_up, L0_ffn_s_down, L1_attn_Wq, L1_attn_Wk, L1_attn_Wv, L1_attn_Ww, L1_attn_cq, L1_attn_ck, L1_attn_cv, L1_attn_Wf1, L1_attn_Wf2, L1_attn_Wb, L1_attn_Wg1, L1_attn_Wg2, L1_attn_bg2, L1_attn_norm_w, L1_attn_Wo, L1_ffn_shared_w1, L1_ffn_shared_b1, L1_ffn_shared_w2, L1_ffn_shared_b2, L1_ffn_routed_w1, L1_ffn_routed_b1, L1_ffn_routed_w2, L1_ffn_routed_b2, L1_ffn_centroids, L1_ffn_bias):

    def _L0_attn_ref(x, wq, wk, wv, conv_q, conv_k, conv_v, wfa, wfb, wb, wga, wgb, a_log, dt_bias, o_norm_w, wo, ln1_w, ln2_w, w_gate, w_up, w_down):
        import jax, jax.numpy as jnp
        import numpy as np
        H, DK, DV = (16, 128, 128)
        EPS = 1e-06

        def _causal_dw_conv(x, w):
            K = w.shape[0]
            T = x.shape[1]
            xp = jnp.pad(x, ((0, 0), (K - 1, 0), (0, 0)))
            out = w[0] * xp[:, 0:T, :]
            for i in range(1, K):
                out = out + w[i] * xp[:, i:i + T, :]
            return out

        def _rmsnorm(h, w):
            hf = h.astype(jnp.float32)
            var = jnp.mean(hf * hf, axis=-1, keepdims=True)
            return (hf * jax.lax.rsqrt(var + EPS)).astype(h.dtype) * w

        def _l2norm(x):
            return x * jax.lax.rsqrt(jnp.sum(x * x, axis=-1, keepdims=True) + EPS)
        B, T, D = x.shape
        h = _rmsnorm(x, ln1_w)
        q = jax.nn.silu(_causal_dw_conv(h @ wq, conv_q)).reshape(B, T, H, DK)
        k = jax.nn.silu(_causal_dw_conv(h @ wk, conv_k)).reshape(B, T, H, DK)
        v = jax.nn.silu(_causal_dw_conv(h @ wv, conv_v)).reshape(B, T, H, DV)
        q = _l2norm(q) * DK ** (-0.5)
        k = _l2norm(k)
        g = -jnp.exp(a_log) * jax.nn.softplus(h @ wfa @ wfb + dt_bias)
        beta = jax.nn.sigmoid(h @ wb)

        def step(S, inp):
            qt, kt, vt, gt, bt = inp
            S = S * jnp.exp(gt)[..., None, None]
            kS = jnp.einsum('bhk,bhkv->bhv', kt, S)
            S = S + bt[..., None, None] * (kt[..., :, None] * (vt - kS)[..., None, :])
            ot = jnp.einsum('bhk,bhkv->bhv', qt, S)
            return (S, ot)
        S0 = jnp.zeros((B, H, DK, DV), x.dtype)
        xs = (q.transpose(1, 0, 2, 3), k.transpose(1, 0, 2, 3), v.transpose(1, 0, 2, 3), g.transpose(1, 0, 2), beta.transpose(1, 0, 2))
        _, o = jax.lax.scan(step, S0, xs)
        o = o.transpose(1, 0, 2, 3)
        gate = (h @ wga @ wgb).reshape(B, T, H, DV)
        o = _rmsnorm(o, o_norm_w) * jax.nn.silu(gate.astype(jnp.float32))
        o = o.astype(x.dtype).reshape(B, T, H * DV) @ wo
        x = x + o
        h2 = _rmsnorm(x, ln2_w)
        mlp = jax.nn.silu(h2 @ w_gate) * (h2 @ w_up) @ w_down
        return x + mlp

    def _L0_ffn_ref(x, w_gate, w_up, w_down, s_gate, s_up, s_down):
        import jax, jax.numpy as jnp
        import numpy as np
        HIDDEN = 256
        INTER = 1024
        B, S = (4, 128)

        def _qmatmul(x, w_int8, scale):
            y = jnp.einsum('bsh,ho->bso', x, w_int8.astype(x.dtype))
            return y * scale
        gate = jax.nn.silu(_qmatmul(x, w_gate, s_gate))
        up = _qmatmul(x, w_up, s_up)
        fuse = gate * up
        return _qmatmul(fuse, w_down, s_down)

    def _L1_attn_ref(hidden_states, Wq, Wk, Wv, Ww, cq, ck, cv, Wf1, Wf2, Wb, Wg1, Wg2, bg2, norm_w, Wo):
        import jax, jax.numpy as jnp
        import numpy as np
        B, T, HID = (1, 128, 256)
        H, DK, DV, M, KW = (16, 128, 128, 128, 4)
        SCALE = DK ** (-0.5)
        EPS = 1e-05

        def short_conv(x, w):
            K = w.shape[1]
            xp = jnp.pad(x, ((0, 0), (K - 1, 0), (0, 0)))
            t = x.shape[1]
            y = sum((xp[:, i:i + t] * w[:, i] for i in range(K)))
            return jax.nn.silu(y)

        def l2norm(x):
            return x * jax.lax.rsqrt(jnp.sum(x * x, axis=-1, keepdims=True) + 1e-06)

        def gsa2_scan(q, k, v, w, g, beta):
            b = q.shape[0]
            tm = lambda x: jnp.moveaxis(x, 1, 0)
            Sk0 = jnp.zeros((b, H, DK, M), q.dtype)
            Sv0 = jnp.zeros((b, H, M, DV), q.dtype)

            def step(carry, xs):
                Sk, Sv = carry
                q_t, k_t, v_t, w_t, g_t, b_t = xs
                gt = jnp.exp(g_t)
                bw = b_t[:, :, None] * w_t
                Sk = Sk * gt[:, :, None, :] + k_t[..., :, None] * bw[:, :, None, :]
                Sv = Sv * gt[..., None] + bw[..., None] * v_t[:, :, None, :]
                s = jnp.einsum('bhd,bhdm->bhm', q_t, Sk) * SCALE
                a = jax.nn.softmax(s, axis=-1)
                o_t = jnp.einsum('bhm,bhmd->bhd', a, Sv)
                return ((Sk, Sv), o_t)
            (_, _), o = jax.lax.scan(step, (Sk0, Sv0), (tm(q), tm(k), tm(v), tm(w), tm(g), tm(beta)))
            return jnp.moveaxis(o, 0, 1)
        h = hidden_states
        q = short_conv(h @ Wq, cq)
        k = short_conv(h @ Wk, ck)
        v = short_conv(h @ Wv, cv)
        w = short_conv(h @ Ww, cv)
        g = jax.nn.log_sigmoid(h @ Wf1 @ Wf2)
        beta = jax.nn.sigmoid(h @ Wb)
        rs = lambda x, d: x.reshape(x.shape[0], x.shape[1], -1, d)
        q, k = (rs(q, DK), rs(k, DK))
        v = rs(v, DV)
        w = l2norm(rs(w, M))
        g = rs(g, M)
        o = gsa2_scan(q, k, v, w, g, beta)
        gate = rs(h @ Wg1 @ Wg2 + bg2, DV)
        o = o * jax.lax.rsqrt(jnp.mean(o * o, axis=-1, keepdims=True) + EPS)
        o = o * norm_w * jax.nn.sigmoid(gate)
        o = o.reshape(o.shape[0], o.shape[1], -1)
        return o @ Wo

    def _L1_ffn_ref(u, shared_w1, shared_b1, shared_w2, shared_b2, routed_w1, routed_b1, routed_w2, routed_b2, centroids, bias):
        import jax, jax.numpy as jnp
        import numpy as np
        D_MODEL, D_FF, NS, NR, KR = (256, 176, 2, 16, 4)
        B, S = (4, 256)

        def _moe_forward(u, shared_w1, shared_b1, shared_w2, shared_b2, routed_w1, routed_b1, routed_w2, routed_b2, centroids, bias):
            b, s, d = u.shape
            flat = u.reshape(-1, d)
            T = flat.shape[0]
            h = jax.nn.relu(jnp.einsum('td,ndf->ntf', flat, shared_w1) + shared_b1[:, None, :])
            shared_out = jnp.einsum('ntf,nfd->td', h, shared_w2) + shared_b2.sum(0)
            out = flat + shared_out
            scores = jax.nn.sigmoid(flat @ centroids.T) + bias
            vals, idx = jax.lax.top_k(scores, KR)
            gating = jnp.zeros_like(scores).at[jnp.arange(T)[:, None], idx].set(vals)
            gating = gating / jnp.clip(gating.sum(-1, keepdims=True), 1e-08)

            def step(acc, ew):
                w1, b1, w2, b2, g = ew
                hj = jax.nn.relu(flat @ w1 + b1)
                yj = hj @ w2 + b2
                return (acc + yj * g[:, None], None)
            rout0 = jnp.zeros_like(flat)
            rout, _ = jax.lax.scan(step, rout0, (routed_w1, routed_b1, routed_w2, routed_b2, gating.T))
            return (out + rout).reshape(b, s, d)
        return _moe_forward(u, shared_w1, shared_b1, shared_w2, shared_b2, routed_w1, routed_b1, routed_w2, routed_b2, centroids, bias)
    x = L0_attn_x
    x = _layernorm(x + _L0_attn_ref(x, L0_attn_wq, L0_attn_wk, L0_attn_wv, L0_attn_conv_q, L0_attn_conv_k, L0_attn_conv_v, L0_attn_wfa, L0_attn_wfb, L0_attn_wb, L0_attn_wga, L0_attn_wgb, L0_attn_a_log, L0_attn_dt_bias, L0_attn_o_norm_w, L0_attn_wo, L0_attn_ln1_w, L0_attn_ln2_w, L0_attn_w_gate, L0_attn_w_up, L0_attn_w_down), axis=-1)
    x = _layernorm(x + _L0_ffn_ref(x, L0_ffn_w_gate, L0_ffn_w_up, L0_ffn_w_down, L0_ffn_s_gate, L0_ffn_s_up, L0_ffn_s_down), axis=-1)
    x = _layernorm(x + _L1_attn_ref(x, L1_attn_Wq, L1_attn_Wk, L1_attn_Wv, L1_attn_Ww, L1_attn_cq, L1_attn_ck, L1_attn_cv, L1_attn_Wf1, L1_attn_Wf2, L1_attn_Wb, L1_attn_Wg1, L1_attn_Wg2, L1_attn_bg2, L1_attn_norm_w, L1_attn_Wo), axis=-1)
    x = _layernorm(x + _L1_ffn_ref(x, L1_ffn_shared_w1, L1_ffn_shared_b1, L1_ffn_shared_w2, L1_ffn_shared_b2, L1_ffn_routed_w1, L1_ffn_routed_b1, L1_ffn_routed_w2, L1_ffn_routed_b2, L1_ffn_centroids, L1_ffn_bias), axis=-1)
    return x

_drawn_inputs = setup_inputs


def setup_inputs(seed=0):
    import zlib

    import numpy as np

    out = dict(_drawn_inputs(seed))
    spreads = {'L0_attn_dt_bias': (1.0, 0.6),
     'L0_attn_o_norm_w': (1.0, 0.6),
     'L0_attn_ln1_w': (1.0, 0.6),
     'L0_attn_ln2_w': (1.0, 0.6),
     'L1_attn_bg2': (0.0, 0.8),
     'L1_attn_norm_w': (1.0, 0.6),
     'L1_ffn_shared_b1': (0.0, 0.1),
     'L1_ffn_shared_b2': (0.0, 0.1),
     'L1_ffn_routed_b1': (0.0, 0.519),
     'L1_ffn_routed_b2': (0.0, 0.355),
     'L1_ffn_bias': (0.0, 0.1)}
    factors = {'L0_attn_wq': 4.752,
     'L0_attn_wk': 5.109,
     'L0_attn_wv': 4.72,
     'L0_attn_conv_q': 4.724,
     'L0_attn_conv_k': 4.524,
     'L0_attn_conv_v': 4.85,
     'L0_attn_wfa': 8.0,
     'L0_attn_wfb': 8.0,
     'L0_attn_wb': 8.0,
     'L0_attn_wga': 4.844,
     'L0_attn_wgb': 4.46,
     'L0_attn_a_log': 8.0,
     'L0_attn_wo': 4.922,
     'L1_attn_Wq': 8.0,
     'L1_attn_Wk': 8.0,
     'L1_attn_cq': 8.0,
     'L1_attn_ck': 8.0,
     'L1_attn_Wf1': 8.0,
     'L1_attn_Wf2': 8.0,
     'L1_attn_Wb': 4.229,
     'L1_attn_Wg1': 8.0,
     'L1_attn_Wg2': 8.0}
    for name, (base, spread) in spreads.items():
        noise = np.random.default_rng([zlib.crc32(name.encode()), seed]).standard_normal(out[name].shape)
        drawn = base * np.exp(spread * noise) if base else spread * noise
        out[name] = jnp.asarray(drawn.astype(out[name].dtype))
    for name, factor in factors.items():
        out[name] = (out[name] * factor).astype(out[name].dtype)
    return out
```

```python
from contextlib import ExitStack

import numpy as np

import concourse.bass as bass
from concourse import mybir

F32 = mybir.dt.float32
U32 = mybir.dt.uint32
I8 = mybir.dt.int8
I32 = mybir.dt.int32
ALU = mybir.AluOpType
ACT = mybir.ActivationFunctionType
AX = mybir.AxisListType

P = 128
B, T, D = 8, 256, 256
NT = B * T // P
KD = D // P
H = 16
HG = 4
NG = H // HG
U = 2 * HG
NL = 7
INTER = 1024
NE, NS, DFF, TOPK = 16, 2, 176, 4
EXP_LN = "natural_log_exp_and_others"
SCALE = float(P) ** -0.5


def shape_constants():
    s = np.arange(P)[:, None]
    t = np.arange(P)[None, :]
    mats = [s == t, s <= t, s > t, np.ones((P, P))]
    for level in range(NL):
        half = 1 << level
        same = (s // (2 * half)) == (t // (2 * half))
        mats.append(same & (s % (2 * half) < half) & (t % (2 * half) >= half))
    for level in range(NL):
        half = 1 << level
        mid = (t // (2 * half)) * 2 * half + half
        mats.append(np.where(t >= mid, (s >= mid) & (s <= t), (s > t) & (s < mid)))
    squares = np.stack([np.asarray(m, np.float32) for m in mats], 1)
    f = np.arange(NE * DFF)[None, :]
    expert = np.asarray(f // DFF == np.arange(NE)[:, None], np.float32)
    return np.ascontiguousarray(squares), expert


class Chip:

    def __init__(self, nc, ctx, io):
        self.nc, self.ctx, self.io = nc, ctx, io
        self.sems = []
        self.x = self.sb("x_tiles", [P, NT, D])
        self.xs = self.sb("xs", [P, NT, D])
        self.hT = self.sb("hT", [P, KD, NT * P])
        self.squares = self.sb("square_mats", [P, 4 + 2 * NL, P])
        self.psum = ctx.enter_context(nc.psum_tensor("psum", [P, 8, 512], F32))
        self.ident = self.squares[:, 0, :]
        self.upper = self.squares[:, 1, :]
        self.lower = self.squares[:, 2, :]
        self.ones = self.squares[:, 3, :]

    def sb(self, name, shape, dt=F32, ctx=None):
        return (ctx or self.ctx).enter_context(self.nc.sbuf_tensor(name, shape, dt))

    def sem(self, name):
        self.sems.append(self.nc.alloc_semaphore(name=name))
        return self.sems[-1]

    def renew_sems(self):
        self.nc.clear_and_free_semaphores(self.sems)
        self.sems = []
        self.nc.all_engine_barrier()

    def pair_mask(self, level):
        return self.squares[:, 4 + level, :]

    def level_sums(self, level):
        return self.squares[:, 4 + NL + level, :]

    def banks(self, first, count, width=None):
        v = self.psum[:, first:first + count, :].rearrange("p b n -> p (b n)")
        return v if width is None else v.rearrange("p (u n) -> p u n", n=width)


def load_stage(c):
    nc, io = c.nc, c.io
    loaded = c.sem("loaded")
    with nc.Block() as block:
        @block.sync
        def _(sp):
            src = io["L0_attn_x"].rearrange("b (c p) d -> p (b c) d", p=P)
            sp.dma_start(c.x[:, :, :], src).then_inc(loaded, 16)
            sp.dma_start(c.squares[:, :, :], io["squares"]).then_inc(loaded, 16)
            sp.dma_start(c.xs[:, :, :], src).then_inc(loaded, 16)
            sp.wait_ge(loaded, 48)


def norm_stage(c, name, rms, plus_x, weight, eps, to_out=False):
    nc = c.nc
    step_tiles = 4
    steps = NT // step_tiles
    with ExitStack() as own:
        stats = c.sb(name + "_stats", [P, step_tiles, 6], ctx=own)
        moments = c.sb(name + "_moments", [P, step_tiles, 2], ctx=own)
        logs = c.sb(name + "_logs", [P, step_tiles], ctx=own)
        rstd = c.sb(name + "_rstd", [P, step_tiles], ctx=own)
        normed = c.sb(name + "_normed", [P, step_tiles, D], ctx=own)
        w_col = c.sb(name + "_w_col", [P, KD], ctx=own)
        w_loaded = c.sem(name + "_w_loaded")
        summed = c.sem(name + "_summed")
        stats_done = c.sem(name + "_stats_done")
        moments_done = c.sem(name + "_moments_done")
        eps_added = c.sem(name + "_eps_added")
        log_done = c.sem(name + "_log_done")
        rstd_done = c.sem(name + "_rstd_done")
        normed_done = c.sem(name + "_normed_done")
        turned = c.sem(name + "_turned")
        stored = c.sem(name + "_stored")
        out_sent = c.sem(name + "_out_sent")

        with nc.Block() as block:
            @block.sync
            def _(sp):
                if weight is not None:
                    with nc.allow_non_contiguous_dma("one column of 128 weights per tile of the width"):
                        sp.dma_start(w_col[:, :], weight.rearrange("(k p) -> p k", p=P)).then_inc(w_loaded, 16)
                if to_out:
                    for g in range(steps):
                        sp.wait_ge(normed_done, step_tiles * (g + 1))
                        sp.dma_start(c.io["out"][:, slice(step_tiles * g, step_tiles * (g + 1)), :],
                                     normed[:, :, :]).then_inc(out_sent, 16)
                    sp.wait_ge(out_sent, 16 * steps)

            @block.vector
            def _(dve):
                for g in range(steps):
                    tiles = slice(step_tiles * g, step_tiles * (g + 1))
                    if plus_x:
                        nc.vector.tensor_tensor(c.xs[:, tiles, :], c.xs[:, tiles, :], c.x[:, tiles, :],
                                                ALU.add).then_inc(summed, 1)
                        dve.wait_ge(summed, g + 1)
                    for j in range(step_tiles):
                        nc.vector.bn_stats(stats[:, j, :], c.xs[:, step_tiles * g + j, :]
                                           ).then_inc(stats_done, 1)
                    dve.wait_ge(stats_done, step_tiles * (g + 1))
                    for j in range(step_tiles):
                        nc.vector.bn_aggr(moments[:, j, :], stats[:, j, :]).then_inc(moments_done, 1)
                    dve.wait_ge(moments_done, step_tiles * (g + 1))
                    if rms:
                        nc.vector.tensor_tensor(logs[:, :], moments[:, :, 0], moments[:, :, 0],
                                                ALU.mult).then_inc(eps_added, 1)
                        dve.wait_ge(eps_added, 2 * g + 1)
                        nc.vector.scalar_tensor_tensor(logs[:, :], logs[:, :], eps, moments[:, :, 1],
                                                       ALU.add, ALU.add).then_inc(eps_added, 1)
                    else:
                        nc.vector.tensor_scalar(logs[:, :], moments[:, :, 1], eps, None,
                                                ALU.add).then_inc(eps_added, 2)
                    dve.wait_ge(rstd_done, g + 1)
                    dve.wait_ge(stored, 3 * g)
                    if to_out:
                        dve.wait_ge(out_sent, 16 * g)
                    for j in range(step_tiles):
                        row = c.xs[:, step_tiles * g + j, :]
                        if rms:
                            op = nc.vector.tensor_scalar(normed[:, j, :], row, rstd[:, j:j + 1], None, ALU.mult)
                        else:
                            op = nc.vector.tensor_scalar(normed[:, j, :], row, moments[:, j, 0:1],
                                                         rstd[:, j:j + 1], ALU.subtract, ALU.mult)
                        op.then_inc(normed_done, 1)

            @block.scalar
            def _(act):
                nc.scalar.preload_act_table_set(EXP_LN)
                if weight is not None:
                    act.wait_ge(w_loaded, 16)
                for g in range(steps):
                    act.wait_ge(eps_added, 2 * (g + 1))
                    nc.scalar.activation(logs[:, :], logs[:, :], ACT.Ln).then_inc(log_done, 1)
                    act.wait_ge(log_done, g + 1)
                    nc.scalar.activation(rstd[:, :], logs[:, :], ACT.Exp, scale=-0.5).then_inc(rstd_done, 1)
                    if to_out:
                        act.sem_inc(stored, 3)
                    else:
                        act.wait_ge(turned, g + 1)
                    for k in range(0 if to_out else KD):
                        scale = 1.0 if weight is None else w_col[:, k:k + 1]
                        nc.scalar.activation(c.hT[:, k, step_tiles * P * g:step_tiles * P * (g + 1)],
                                             c.psum[:, k, :], ACT.Copy, scale=scale).then_inc(stored, 1)

            @block.tensor
            def _(pe):
                if to_out:
                    return
                for g in range(steps):
                    pe.wait_ge(normed_done, step_tiles * (g + 1))
                    pe.wait_ge(stored, 3 * g)
                    for k in range(KD):
                        for j in range(step_tiles):
                            last = nc.tensor.transpose(c.psum[:, k, j * P:(j + 1) * P],
                                                       normed[:, j, k * P:(k + 1) * P], c.ident)
                    last.then_inc(turned, 1)

            @block.gpsimd
            def _(pool):
                if to_out:
                    return
                for g in range(steps):
                    tiles = slice(step_tiles * g, step_tiles * (g + 1))
                    pool.wait_ge(normed_done, step_tiles * (g + 1))
                    if rms:
                        pool.sem_inc(stored, 1)
                    else:
                        nc.gpsimd.tensor_copy(c.x[:, tiles, :], normed[:, :, :])
                        nc.gpsimd.tensor_copy(c.xs[:, tiles, :], normed[:, :, :]).then_inc(stored, 1)


def narrow_stage(c, name, w_f, w_g, w_b, f_T, g_T, beta):
    nc = c.nc
    with ExitStack() as own:
        w_f_sb = c.sb(name + "_w_f", [P, KD, P], ctx=own)
        w_g_sb = c.sb(name + "_w_g", [P, KD, P], ctx=own)
        w_b_sb = c.sb(name + "_w_b", [P, KD, H], ctx=own)
        exp_b = c.sb(name + "_exp_b", [P, NT * H], ctx=own)
        loaded = c.sem(name + "_loaded")
        f_done = c.sem(name + "_f_done")
        b_done = c.sem(name + "_b_done")
        g_done = c.sem(name + "_g_done")
        copied = c.sem(name + "_copied")
        exp_done = c.sem(name + "_exp_done")
        beta_step = c.sem(name + "_beta_step")
        with nc.Block() as block:
            @block.sync
            def _(sp):
                sp.dma_start(w_f_sb[:, :, :], w_f.rearrange("(k p) n -> p k n", p=P)).then_inc(loaded, 16)
                sp.dma_start(w_g_sb[:, :, :], w_g.rearrange("(k p) n -> p k n", p=P)).then_inc(loaded, 16)
                sp.dma_start(w_b_sb[:, :, :], w_b.rearrange("(k p) n -> p k n", p=P)).then_inc(loaded, 16)

            @block.tensor
            def _(pe):
                pe.wait_ge(loaded, 48)
                for q in range(4):
                    for k in range(KD):
                        last = nc.tensor.matmul(c.psum[:, q, :], w_f_sb[:, k, :], c.hT[:, k, q * 512:(q + 1) * 512],
                                                start=k == 0, stop=k == KD - 1)
                last.then_inc(f_done, 1)
                for n in range(NT):
                    for k in range(KD):
                        last = nc.tensor.matmul(c.psum[:, 4, n * H:(n + 1) * H], c.hT[:, k, n * P:(n + 1) * P],
                                                w_b_sb[:, k, :], start=k == 0, stop=k == KD - 1)
                last.then_inc(b_done, 1)
                pe.wait_ge(copied, 1)
                for q in range(4):
                    for k in range(KD):
                        last = nc.tensor.matmul(c.psum[:, q, :], w_g_sb[:, k, :], c.hT[:, k, q * 512:(q + 1) * 512],
                                                start=k == 0, stop=k == KD - 1)
                last.then_inc(g_done, 1)

            @block.scalar
            def _(act):
                act.wait_ge(f_done, 1)
                nc.scalar.activation(f_T[:, :], c.banks(0, 4), ACT.Copy).then_inc(copied, 1)
                act.wait_ge(b_done, 1)
                nc.scalar.activation(exp_b[:, :], c.psum[:, 4, 0:NT * H], ACT.Exp, scale=-1.0).then_inc(exp_done, 1)
                act.wait_ge(g_done, 1)
                nc.scalar.activation(g_T[:, :], c.banks(0, 4), ACT.Copy).then_inc(copied, 1)

            @block.vector
            def _(dve):
                dve.wait_ge(exp_done, 1)
                nc.vector.tensor_scalar_add(exp_b[:, :], exp_b[:, :], 1.0).then_inc(beta_step, 1)
                dve.wait_ge(beta_step, 1)
                for g in range(NG):
                    nc.vector.reciprocal(
                        beta[:, g, :, :].rearrange("p b (c h) -> p b c h", c=2),
                        exp_b[:, :].rearrange("p (b c g h) -> p g b c h", b=B, c=2, g=NG)[:, g])


def decay_stage(c, w_fb, dt_bias, a_log, f_T, per_token):
    nc = c.nc
    G, FROM_START, TO_END, WHOLE = range(4)
    with ExitStack() as own:
        w_fb_sb = c.sb("w_fb_sb", [P, H], ctx=own)
        rows = c.sb("bias_rows", [1, 2 * H], ctx=own)
        bias = c.sb("bias_bc", [P, H], ctx=own)
        rate = c.sb("decay_rate", [P, H], ctx=own)
        y = c.sb("decay_y", [P, NT * H], ctx=own)
        log1p = c.sb("decay_log1p", [P, NT * H], ctx=own)
        g = c.sb("decay_g", [P, NT * H], ctx=own)
        loaded = c.sem("decay_loaded")
        f_done = c.sem("decay_f_done")
        rate_step = c.sem("rate_step")
        y_done = c.sem("decay_y_done")
        soft = c.sem("decay_soft")
        g_done = c.sem("decay_g_done")
        sums_done = c.sem("decay_sums_done")

        def by_head(v):
            return v.rearrange("p (n h) -> p n h", h=H)

        def group_view(v, g):
            return v.rearrange("p (b c g h) -> p g b c h", b=B, c=2, g=NG)[:, g]

        with nc.Block() as block:
            @block.sync
            def _(sp):
                sp.dma_start(w_fb_sb[:, :], w_fb).then_inc(loaded, 16)
                sp.dma_start(rows[:, 0:H], dt_bias.rearrange("(a n) -> a n", a=1)).then_inc(loaded, 16)
                sp.dma_start(rows[:, H:2 * H], a_log.rearrange("(a n) -> a n", a=1)).then_inc(loaded, 16)

            @block.tensor
            def _(pe):
                pe.wait_ge(loaded, 48)
                nc.tensor.matmul(c.psum[:, 1, 0:2 * H], c.ones[0:1, :], rows[:, :], start=True, stop=True)
                for n in range(NT):
                    last = nc.tensor.matmul(c.psum[:, 0, n * H:(n + 1) * H], f_T[:, n * P:(n + 1) * P],
                                            w_fb_sb[:, :], start=True, stop=True)
                last.then_inc(f_done, 1)
                pe.wait_ge(g_done, 1)
                for n, sums in enumerate((c.upper, c.lower, c.ones)):
                    last = nc.tensor.matmul(c.psum[:, 2 + n, 0:NT * H], sums, g[:, :], start=True, stop=True)
                last.then_inc(sums_done, 1)

            @block.vector
            def _(dve):
                dve.wait_ge(f_done, 1)
                nc.vector.tensor_copy(bias[:, :], c.psum[:, 1, 0:H]).then_inc(rate_step, 1)
                dve.wait_ge(rate_step, 1)
                nc.vector.tensor_tensor(by_head(y[:, :]), by_head(c.psum[:, 0, 0:NT * H]),
                                        bias[:, :].unsqueeze(1).broadcast_to([P, NT, H]), ALU.add).then_inc(y_done, 1)
                dve.wait_ge(soft, 4)
                nc.vector.scalar_tensor_tensor(y[:, :], y[:, :], 0.0, log1p[:, :], ALU.max, ALU.add
                                               ).then_inc(y_done, 1)
                dve.wait_ge(y_done, 2)
                nc.vector.scalar_tensor_tensor(by_head(g[:, :]), by_head(y[:, :]), -1.0,
                                               rate[:, :].unsqueeze(1).broadcast_to([P, NT, H]),
                                               ALU.mult, ALU.mult).then_inc(g_done, 1)
                dve.wait_ge(g_done, 1)
                for n in range(NG):
                    nc.vector.tensor_copy(per_token[:, G, n, :, :].rearrange("p b (c h) -> p b c h", c=2),
                                          group_view(g[:, :], n))

            @block.scalar
            def _(act):
                act.wait_ge(y_done, 1)
                nc.scalar.activation(rate[:, :], c.psum[:, 1, H:2 * H], ACT.Exp).then_inc(soft, 1)
                nc.scalar.activation(log1p[:, :], y[:, :], ACT.Abs).then_inc(soft, 1)
                act.wait_ge(soft, 2)
                nc.scalar.activation(log1p[:, :], log1p[:, :], ACT.Exp, scale=-1.0).then_inc(soft, 1)
                act.wait_ge(soft, 3)
                nc.scalar.activation(log1p[:, :], log1p[:, :], ACT.Ln, bias=1.0).then_inc(soft, 1)
                act.wait_ge(sums_done, 1)
                for n, k in enumerate((FROM_START, TO_END, WHOLE)):
                    for i in range(NG):
                        nc.scalar.activation(per_token[:, k, i, :, :].rearrange("p b (c h) -> p b c h", c=2),
                                             group_view(c.psum[:, 2 + n, 0:NT * H], i), ACT.Exp)


def delta_stage(c, io, gate_T, per_token):
    nc = c.nc
    G, FROM_START, TO_END, WHOLE, BETA = range(5)
    Q, K, V = range(3)
    TAPS = 4
    STEPS = NG * B
    with ExitStack() as own:
        def sb(name, shape):
            return c.sb("d_" + name, shape, ctx=own)

        def sem(name):
            return c.sem("d_" + name)

        conv_all = sb("conv_all", [P, 3, TAPS, H])
        conv = sb("conv", [P, 3, TAPS, HG])
        norm_w = sb("norm_w", [P, 1])
        w_qkv = sb("w_qkv", [P, 3, KD, HG * P])
        w_gate = sb("w_gate", [P, HG * P])
        w_o = sb("w_o", [P, HG, D])
        tok = sb("tok", [P, 5, U])
        pre = sb("pre", [P, 3, HG, T + TAPS - 1])
        qkv = sb("qkv", [P, 3, HG, T])
        gate = sb("gate", [P, HG, T])
        sq = sb("sq", [P, 2, HG, T])
        k_tok = sb("k_tok", [P, U, P])
        v_tok = sb("v_tok", [P, U, P])
        g_cols = sb("g_cols", [P, U, P])
        decay = sb("decay", [P, U, P])
        scores = sb("scores", [P, U, P])
        a_all = sb("a_all", [P, U, P])
        RING = 3
        a_level = sb("a_level", [P, RING, U, P])
        X = sb("X", [P, U, P])
        XT = sb("XT", [P, U, P])
        y = sb("y", [P, U, P])
        u = sb("u", [P, U, P])
        u_end = sb("u_end", [P, HG, P])
        state = sb("state", [P, HG, P])
        rest = sb("rest", [P, HG, P])
        from_state = sb("from_state", [P, HG, P])
        o = sb("o", [P, U, P])
        oT = sb("oT", [P, U, P])
        sums = sb("sums", [P, 2, U])
        logs = sb("logs", [P, 2, U])
        q_scale = sb("q_scale", [P, U])
        k_norm = sb("k_norm", [P, U])
        b = sb("b", [P, U])
        minus_start = sb("minus_start", [P, U])
        o_sums = sb("o_sums", [P, U])
        o_scale = sb("o_scale", [P, U])
        conv_rows = own.enter_context(nc.sbuf_tensor("d_conv_rows", [TAPS * H, 3, P], F32))

        x_place = c.x[:, :, :].rearrange("p n d -> p (n d)").rearrange("p (w h t) -> p w h t", w=4, t=T)
        x_in = sem("x_in")
        w_o_in = sem("w_o_in")
        gate_copied = sem("gate_copied")
        taps_ready = sem("taps_ready")
        pre_padded = sem("pre_padded")
        XT_masked = sem("XT_masked")
        scores_read = sem("scores_read")
        scores_ready = sem("scores_ready")
        consts_in = sem("consts_in")
        conv_turned = sem("conv_turned")
        conv_ready = sem("conv_ready")
        weights_in = sem("weights_in")
        tok_ready = sem("tok_ready")
        projected = sem("projected")
        pre_ready = sem("pre_ready")
        conv_step = sem("conv_step")
        silu_done = sem("silu_done")
        squared = sem("squared")
        kv_turned = sem("kv_turned")
        kv_copied = sem("kv_copied")
        scored = sem("scored")
        g_cols_ready = sem("g_cols_ready")
        decay_summed = sem("decay_summed")
        decay_ready = sem("decay_ready")
        sq_summed = sem("sq_summed")
        eps_added = sem("eps_added")
        log_done = sem("log_done")
        norms_ready = sem("norms_ready")
        b_ready = sem("b_ready")
        v_scaled = sem("v_scaled")
        a_ready = sem("a_ready")
        level_masked = sem("level_masked")
        XT_first = sem("XT_first")
        X_turned = sem("X_turned")
        X_first = sem("X_first")
        y_done = sem("y_done")
        y_copied = sem("y_copied")
        z_done = sem("z_done")
        X_step = sem("X_step")
        w_done = sem("w_done")
        u_ready = sem("u_ready")
        u_end_ready = sem("u_end_ready")
        within_done = sem("within_done")
        state_done = sem("state_done")
        state_ready = sem("state_ready")
        from_state_done = sem("from_state_done")
        from_state_ready = sem("from_state_ready")
        rest_ready = sem("rest_ready")
        o_ready = sem("o_ready")
        o_squared = sem("o_squared")
        o_eps = sem("o_eps")
        o_log = sem("o_log")
        o_rstd = sem("o_rstd")
        o_scale_ready = sem("o_scale_ready")
        o_normed = sem("o_normed")
        o_turned = sem("o_turned")
        o_gated = sem("o_gated")
        out_done = sem("out_done")
        added = sem("added")

        def bank_of(unit, first):
            return c.psum[:, first + unit // HG, (unit % HG) * P:(unit % HG + 1) * P]

        def chunk(w, unit):
            return qkv[:, w, unit % HG, (unit // HG) * P:(unit // HG + 1) * P]

        X_STEPS = 2 * 2 * (NL - 2) + 2

        def x_steps(level, half):
            per = 2 if level < NL - 1 else 1
            return 4 * (level - 1) + per * (half + 1)

        def conv_in(w):
            return x_place[:, w, :, :]

        with nc.Block() as block:
            @block.sync
            def _(sp):
                for w, name in enumerate(("q", "k", "v")):
                    sp.dma_start(conv_rows[:, w, :], io["L0_attn_conv_" + name].rearrange("a (h p) -> (a h) p", p=P)
                                 ).then_inc(consts_in, 16)
                sp.dma_start(norm_w[:, :], io["L0_attn_o_norm_w"].rearrange("(p a) -> p a", a=1)
                             ).then_inc(consts_in, 16)

                def load_in(group):
                    heads = bass.ds(group * (HG * P), HG * P)
                    for w, name in enumerate(("wq", "wk", "wv")):
                        sp.dma_start(w_qkv[:, w, :, :], io["L0_attn_" + name].rearrange("(k p) n -> p k n", p=P)[:, :, heads]
                                     ).then_inc(weights_in, 16)
                    sp.dma_start(w_gate[:, :], io["L0_attn_wgb"][:, heads]).then_inc(weights_in, 16)

                def load_out(group):
                    sp.dma_start(w_o[:, :, :], io["L0_attn_wo"].rearrange("(g h p) n -> p g h n", p=P, h=HG)
                                 [:, bass.ds(group, 1), :, :]).then_inc(w_o_in, 16)

                load_in(0)
                load_out(0)
                with sp.Fori(1, NG) as hg:
                    sp.wait_ge(projected, 4 * B * hg)
                    load_in(hg)
                    sp.wait_ge(out_done, 2 * B * hg)
                    load_out(hg)
                sp.wait_ge(silu_done, 4 * STEPS)
                sp.dma_start(c.x[:, :, :], io["L0_attn_x"].rearrange("b (c p) d -> p (b c) d", p=P)).then_inc(x_in, 16)
                sp.wait_ge(x_in, 16)

            @block.tensor
            def _(pe):
                def project(w, m):
                    if w == 0:
                        pe.wait_ge(weights_in, 64 * (m // B) + 64)
                    else:
                        pe.wait_ge(pre_ready, 3 * m + w)
                    tokens = bass.ds((m % B) * T, T)
                    for h in range(HG):
                        out = c.psum[:, 2 + h // 2, (h % 2) * T:(h % 2 + 1) * T]
                        if w == 3:
                            last = nc.tensor.matmul(out, w_gate[:, h * P:(h + 1) * P], gate_T[:, tokens],
                                                    start=True, stop=True)
                        else:
                            for k in range(KD):
                                last = nc.tensor.matmul(out, w_qkv[:, w, k, h * P:(h + 1) * P], c.hT[:, k, tokens],
                                                        start=k == 0, stop=k == KD - 1)
                    last.then_inc(projected, 1)

                def step(n, ahead):
                    pe.wait_ge(g_cols_ready, n + 1)
                    for half in range(2):
                        last = nc.tensor.matmul(c.psum[:, half, :], c.lower,
                                                g_cols[:, half * HG:(half + 1) * HG, :], start=True, stop=True)
                    last.then_inc(decay_summed, 1)
                    pe.wait_ge(silu_done, 4 * n + 2)
                    for i in range(U):
                        last = nc.tensor.matmul(c.psum[:, 4 + i // 2, (i % 2) * 2 * P:(i % 2 + 1) * 2 * P], chunk(K, i),
                                                qkv[:, 0:2, i % HG, (i // HG) * P:(i // HG + 1) * P],
                                                start=True, stop=True)
                    last.then_inc(scored, 1)
                    pe.wait_ge(silu_done, 4 * n + 3)
                    pe.wait_ge(added, n + 1)
                    for i in range(U):
                        last = nc.tensor.transpose(bank_of(i, 2), chunk(V, i), c.ident)
                    last.then_inc(kv_turned, 1)
                    pe.wait_ge(decay_ready, n + 1)
                    for i in range(U):
                        last = nc.tensor.transpose(bank_of(i, 0), chunk(K, i), c.ident)
                    last.then_inc(kv_turned, 1)
                    pe.wait_ge(kv_copied, 2 * n + 1)
                    pe.wait_ge(squared, n + 1)
                    for w in range(2):
                        for i in range(U):
                            last = nc.tensor.matmul(c.psum[:, 2, w * U + i:w * U + i + 1],
                                                    sq[:, w, i % HG, (i // HG) * P:(i // HG + 1) * P],
                                                    c.ones[:, 0:1], start=True, stop=True)
                    last.then_inc(sq_summed, 1)
                    for half in range(2):
                        pe.wait_ge(XT_first, 2 * n + half + 1)
                        for i in range(half * HG, (half + 1) * HG):
                            last = nc.tensor.transpose(bank_of(i, 2), XT[:, i, :], c.ident)
                        last.then_inc(X_turned, 1)
                    pe.wait_ge(scores_read, n + 1)
                    for level in range(1, NL):
                        pe.wait_ge(level_masked, (NL - 1) * n + level)
                        for half in range(2):
                            if level > 1:
                                pe.wait_ge(X_step, X_STEPS * n + x_steps(level - 1, half))
                            else:
                                pe.wait_ge(X_first, 2 * n + half + 1)
                            for i in range(half * HG, (half + 1) * HG):
                                last = nc.tensor.matmul(bank_of(i, 4), a_level[:, level % RING, i, :], X[:, i, :],
                                                        start=True, stop=True)
                            last.then_inc(y_done, 1)
                        if ahead and level <= 4:
                            project(level - 1, n + 1)
                        for half in range(2):
                            pe.wait_ge(y_copied, 2 * (NL - 1) * n + 2 * (level - 1) + half + 1)
                            if level == 1:
                                pe.wait_ge(kv_copied, 2 * n + 2)
                            if level < NL - 1:
                                for i in range(half * HG, (half + 1) * HG):
                                    nc.tensor.matmul(bank_of(i, 6), XT[:, i, :], y[:, i, :], start=True, stop=True)
                            for i in range(half * HG, (half + 1) * HG):
                                last = nc.tensor.matmul(bank_of(i, 0), y[:, i, :], XT[:, i, :], start=True, stop=True)
                            last.then_inc(z_done, 1)
                    pe.wait_ge(v_scaled, n + 1)
                    if ahead:
                        pe.wait_ge(gate_copied, n + 2)
                    pe.wait_ge(X_step, X_STEPS * n + X_STEPS - 1)
                    for i in range(HG):
                        last = nc.tensor.matmul(bank_of(i, 2), XT[:, i, :], v_tok[:, i, :], start=True, stop=True)
                    last.then_inc(w_done, 1)
                    pe.wait_ge(u_ready, 2 * n + 1)
                    pe.wait_ge(scores_ready, n + 1)
                    for i in range(HG):
                        last = nc.tensor.matmul(bank_of(i, 3), scores[:, i, :], u[:, i, :], start=True, stop=True)
                    last.then_inc(within_done, 1)
                    pe.wait_ge(u_end_ready, n + 1)
                    for i in range(HG):
                        last = nc.tensor.matmul(bank_of(i, 4), k_tok[:, i, :], u_end[:, i, :], start=True, stop=True)
                    last.then_inc(state_done, 1)
                    pe.wait_ge(state_ready, n + 1)
                    for i in range(HG):
                        last = nc.tensor.matmul(bank_of(i, 5), chunk(K, HG + i), state[:, i, :], start=True, stop=True)
                    last.then_inc(from_state_done, 1)
                    for i in range(HG):
                        last = nc.tensor.matmul(bank_of(i, 6), chunk(Q, HG + i), state[:, i, :], start=True, stop=True)
                    last.then_inc(from_state_done, 1)
                    pe.wait_ge(rest_ready, n + 1)
                    pe.wait_ge(X_step, X_STEPS * n + X_STEPS)
                    for i in range(HG):
                        last = nc.tensor.matmul(bank_of(i, 7), XT[:, HG + i, :], rest[:, i, :], start=True, stop=True)
                    last.then_inc(w_done, 1)
                    pe.wait_ge(o_normed, 2 * n + 1)
                    for i in range(HG):
                        last = nc.tensor.transpose(bank_of(i, 1), o[:, i, :], c.ident)
                    last.then_inc(o_turned, 1)
                    pe.wait_ge(u_ready, 2 * n + 2)
                    for i in range(HG):
                        last = nc.tensor.matmul(bank_of(i, 0), scores[:, HG + i, :], u[:, HG + i, :],
                                                start=True, stop=True)
                    last.then_inc(within_done, 1)
                    pe.wait_ge(w_o_in, 16 * (n // B) + 16)
                    for half in range(2):
                        if half:
                            pe.wait_ge(o_normed, 2 * n + 2)
                            for i in range(HG, U):
                                last = nc.tensor.transpose(bank_of(i, 1), o[:, i, :], c.ident)
                            last.then_inc(o_turned, 1)
                        pe.wait_ge(o_gated, 2 * n + half + 2)
                        for h in range(HG):
                            last = nc.tensor.matmul(c.psum[:, 3, half * D:(half + 1) * D], oT[:, half * HG + h, :],
                                                    w_o[:, h, :], start=h == 0, stop=h == HG - 1)
                        last.then_inc(out_done, 1)

                pe.wait_ge(consts_in, 64)
                for w in range(3):
                    last = nc.tensor.transpose(c.psum[:, 0, w * TAPS * H:(w + 1) * TAPS * H], conv_rows[:, w, :],
                                               c.ident[0:TAPS * H, 0:TAPS * H])
                last.then_inc(conv_turned, 1)
                for w in range(4):
                    project(w, 0)
                pe.wait_ge(conv_ready, 1)
                pe.wait_ge(gate_copied, 1)
                with pe.Fori(0, STEPS - 1) as n:
                    step(n, True)
                step(STEPS - 1, False)

            @block.scalar
            def _(act):
                def take(w, m):
                    act.wait_ge(projected, 4 * m + w + 1)
                    if w < 3:
                        nc.scalar.activation(pre[:, w, :, TAPS - 1:], c.banks(2, 2, T), ACT.Copy).then_inc(pre_ready, 1)
                    else:
                        nc.scalar.activation(x_place[:, 3, :, :], c.banks(2, 2, T), ACT.Copy).then_inc(gate_copied, 1)

                def step(n, ahead):
                    act.wait_ge(conv_step, 48 * n + 48)
                    for w in (K, Q, V):
                        nc.scalar.activation(qkv[:, w, :, :], conv_in(w), ACT.Silu).then_inc(silu_done, 1)
                    act.wait_ge(gate_copied, n + 1)
                    act.wait_ge(o_gated, 2 * n + 1)
                    nc.scalar.activation(gate[:, :, :], x_place[:, 3, :, :], ACT.Silu).then_inc(silu_done, 1)
                    nc.scalar.preload_act_table_set(EXP_LN)
                    act.wait_ge(decay_summed, n + 1)
                    nc.scalar.activation(decay[:, :, :], c.banks(0, 2, P), ACT.Exp).then_inc(decay_ready, 1)
                    act.wait_ge(kv_turned, 2 * n + 1)
                    nc.scalar.activation(v_tok[:, :, :], c.banks(2, 2, P), ACT.Copy).then_inc(kv_copied, 1)
                    act.wait_ge(eps_added, n + 1)
                    nc.scalar.activation(logs[:, :, :], sums[:, :, :], ACT.Ln).then_inc(log_done, 1)
                    act.wait_ge(log_done, n + 1)
                    nc.scalar.activation(b[:, :], logs[:, K, :], ACT.Exp, scale=-1.0)
                    nc.scalar.activation(q_scale[:, :], logs[:, Q, :], ACT.Exp, scale=-0.5)
                    nc.scalar.activation(k_norm[:, :], logs[:, K, :], ACT.Exp, scale=0.5).then_inc(norms_ready, 1)
                    act.wait_ge(kv_turned, 2 * n + 2)
                    nc.scalar.activation(k_tok[:, :, :], c.banks(0, 2, P), ACT.Copy).then_inc(kv_copied, 1)
                    for half in range(2):
                        act.wait_ge(X_turned, 2 * n + half + 1)
                        nc.scalar.activation(X[:, half * HG:(half + 1) * HG, :], c.banks(2 + half, 1, P), ACT.Copy
                                             ).then_inc(X_first, 1)
                    for level in range(1, NL):
                        for half in range(2):
                            act.wait_ge(y_done, 2 * (NL - 1) * n + 2 * (level - 1) + half + 1)
                            nc.scalar.activation(y[:, half * HG:(half + 1) * HG, :], c.banks(4 + half, 1, P),
                                                 ACT.Copy).then_inc(y_copied, 1)
                        if ahead and level <= 4:
                            take(level - 1, n + 1)

                    def to_u(half):
                        act.wait_ge(w_done, 2 * n + half + 1)
                        for i in range(half * HG, (half + 1) * HG):
                            last = nc.scalar.activation(u[:, i, :], bank_of(i - half * HG, 7 if half else 2), ACT.Copy,
                                                        scale=b[:, i:i + 1])
                        last.then_inc(u_ready, 1)

                    def squares(half):
                        act.wait_ge(o_ready, 2 * n + half + 1)
                        for i in range(half * HG, (half + 1) * HG):
                            last = nc.scalar.activation(decay[:, i, :], o[:, i, :], ACT.Square, scale=q_scale[:, i:i + 1],
                                                        accum_out=o_sums[:, i:i + 1])
                        last.then_inc(o_squared, 1)

                    def rstd(half):
                        part = o_sums[:, half * HG:(half + 1) * HG]
                        act.wait_ge(o_eps, 2 * n + half + 1)
                        nc.scalar.activation(part, part, ACT.Ln).then_inc(o_log, 1)
                        act.wait_ge(o_log, 2 * n + half + 1)
                        nc.scalar.activation(part, part, ACT.Exp, scale=-0.5).then_inc(o_rstd, 1)

                    def normalise(half):
                        act.wait_ge(o_scale_ready, 2 * n + half + 1)
                        for i in range(half * HG, (half + 1) * HG):
                            last = nc.scalar.activation(o[:, i, :], o[:, i, :], ACT.Copy, scale=o_scale[:, i:i + 1])
                        last.then_inc(o_normed, 1)

                    to_u(0)
                    act.wait_ge(state_done, n + 1)
                    nc.scalar.activation(state[:, :, :], c.banks(4, 1, P), ACT.Copy).then_inc(state_ready, 1)
                    squares(0)
                    rstd(0)
                    normalise(0)
                    act.wait_ge(from_state_done, 2 * n + 2)
                    to_u(1)
                    for i in range(HG):
                        last = nc.scalar.activation(from_state[:, i, :], bank_of(i, 6), ACT.Copy,
                                                    scale=tok[:, FROM_START, HG + i:HG + i + 1])
                    last.then_inc(from_state_ready, 1)
                    squares(1)
                    rstd(1)
                    normalise(1)

                act.wait_ge(conv_turned, 1)
                nc.scalar.activation(conv_all[:, :, :, :], c.psum[:, 0, 0:3 * TAPS * H], ACT.Copy).then_inc(conv_ready, 1)
                for w in range(4):
                    take(w, 0)
                with act.Fori(0, STEPS - 1) as n:
                    step(n, True)
                step(STEPS - 1, False)

            @block.vector
            def _(dve):
                def convolve(k, m):
                    w, tap = k // TAPS, TAPS - 1 - k % TAPS
                    if k == 0:
                        nc.vector.tensor_copy(conv[:, :, :, :], conv_all[:, :, :, bass.ds((m // B) * HG, HG)]
                                              ).then_inc(taps_ready, 1)
                        dve.wait_ge(taps_ready, m + 1)
                    if k % TAPS == 0:
                        dve.wait_ge(pre_ready, 3 * m + w + 1)
                    else:
                        dve.wait_ge(conv_step, 48 * m + 4 * k)
                    for h in range(HG):
                        source = pre[:, w, h, tap:tap + T]
                        weight = conv[:, w, tap, h:h + 1]
                        to = conv_in(w)[:, h, :]
                        if k % TAPS == 0:
                            op = nc.vector.tensor_scalar(to, source, weight, None, ALU.mult)
                        else:
                            op = nc.vector.scalar_tensor_tensor(to, source, weight, to, ALU.mult, ALU.add)
                        op.then_inc(conv_step, 1)

                def step(n, ahead):
                    dve.wait_ge(sq_summed, n + 1)
                    nc.vector.tensor_scalar_add(sums[:, :, :], c.psum[:, 2, 0:2 * U].rearrange("p (w u) -> p w u", w=2),
                                                1e-6).then_inc(eps_added, 1)
                    dve.wait_ge(norms_ready, n + 1)
                    nc.vector.tensor_tensor(b[:, :], b[:, :], tok[:, BETA, :], ALU.mult).then_inc(b_ready, 1)
                    nc.vector.tensor_scalar(q_scale[:, :], q_scale[:, :], SCALE, None, ALU.mult)
                    nc.vector.tensor_scalar(minus_start[:, :], tok[:, FROM_START, :], -1.0, None, ALU.mult)
                    dve.wait_ge(scored, n + 1)
                    dve.wait_ge(decay_ready, n + 1)
                    dve.wait_ge(b_ready, n + 1)
                    both = c.banks(4, 4).rearrange("p (u w n) -> p w u n", w=2, n=P)
                    for i in range(U):
                        nc.vector.scalar_tensor_tensor(a_all[:, i, :], both[:, K, i, :], b[:, i:i + 1],
                                                       decay[:, i, :], ALU.mult, ALU.mult).then_inc(a_ready, 1)
                    for half in range(2):
                        units = slice(half * HG, (half + 1) * HG)
                        dve.wait_ge(a_ready, U * n + (half + 1) * HG)
                        nc.vector.tensor_tensor(XT[:, units, :], a_all[:, units, :],
                                                c.pair_mask(0).unsqueeze(1).broadcast_to([P, HG, P]), ALU.mult
                                                ).then_inc(XT_masked, 1)
                    for half in range(2):
                        units = slice(half * HG, (half + 1) * HG)
                        dve.wait_ge(XT_masked, 2 * n + half + 1)
                        nc.vector.scalar_tensor_tensor(XT[:, units, :], XT[:, units, :], -1.0,
                                                       c.ident.unsqueeze(1).broadcast_to([P, HG, P]),
                                                       ALU.mult, ALU.add).then_inc(XT_first, 1)
                    nc.vector.tensor_tensor(scores[:, :, :], both[:, Q, :, :], decay[:, :, :], ALU.mult
                                            ).then_inc(scores_read, 1)
                    for level in range(1, NL):
                        for half in range(2):
                            dve.wait_ge(z_done, 2 * (NL - 1) * n + 2 * (level - 1) + half + 1)
                            units = slice(half * HG, (half + 1) * HG)
                            if level < NL - 1:
                                nc.vector.tensor_tensor(X[:, units, :], X[:, units, :], c.banks(6 + half, 1, P),
                                                        ALU.subtract).then_inc(X_step, 1)
                            nc.vector.tensor_tensor(XT[:, units, :], XT[:, units, :], c.banks(half, 1, P),
                                                    ALU.subtract).then_inc(X_step, 1)
                            slot = 2 * (level - 1) + half
                            if ahead and slot:
                                convolve(slot - 1, n + 1)
                    if ahead:
                        convolve(2 * (NL - 1) - 1, n + 1)
                    dve.wait_ge(within_done, 2 * n + 1)
                    nc.vector.tensor_copy(o[:, 0:HG, :], c.banks(3, 1, P)).then_inc(o_ready, 1)
                    dve.wait_ge(from_state_done, 2 * n + 1)
                    for i in range(HG):
                        last = nc.vector.scalar_tensor_tensor(rest[:, i, :], bank_of(i, 5),
                                                              minus_start[:, HG + i:HG + i + 1],
                                                              v_tok[:, HG + i, :], ALU.mult, ALU.add)
                    last.then_inc(rest_ready, 1)

                    def scale(half):
                        part = slice(half * HG, (half + 1) * HG)
                        dve.wait_ge(o_squared, 2 * n + half + 1)
                        nc.vector.tensor_scalar(o_sums[:, part], o_sums[:, part], 1.0 / P, 1e-6, ALU.mult, ALU.add
                                                ).then_inc(o_eps, 1)
                        dve.wait_ge(o_rstd, 2 * n + half + 1)
                        nc.vector.tensor_tensor(o_scale[:, part], o_sums[:, part], q_scale[:, part], ALU.mult
                                                ).then_inc(o_scale_ready, 1)

                    def gate_output(half):
                        dve.wait_ge(o_turned, 2 * n + half + 1)
                        nc.vector.scalar_tensor_tensor(oT[:, half * HG:(half + 1) * HG, :], c.banks(1 + half, 1, P),
                                                       norm_w[:, 0:1], gate[:, :, half * P:(half + 1) * P],
                                                       ALU.mult, ALU.mult).then_inc(o_gated, 1)

                    scale(0)
                    gate_output(0)
                    dve.wait_ge(from_state_ready, n + 1)
                    dve.wait_ge(within_done, 2 * n + 2)
                    nc.vector.tensor_tensor(o[:, HG:U, :], from_state[:, :, :], c.banks(0, 1, P), ALU.add
                                            ).then_inc(o_ready, 1)
                    scale(1)
                    if ahead:
                        nc.vector.tensor_copy(tok[:, :, :], by_step[:, :, bass.ds(n + 1, 1), :]).then_inc(tok_ready, 1)
                    gate_output(1)
                    dve.wait_ge(out_done, 2 * n + 2)
                    seq = n % B
                    nc.vector.tensor_tensor(c.xs[:, bass.ds(2 * seq, 2), :], c.xs[:, bass.ds(2 * seq, 2), :],
                                            c.banks(3, 1, D), ALU.add).then_inc(added, 1)

                dve.sem_inc(added, 1)
                dve.sem_inc(o_gated, 1)
                by_step = per_token.rearrange("p a g b u -> p a (g b) u")
                nc.vector.tensor_copy(tok[:, :, :], by_step[:, :, 0:1, :]).then_inc(tok_ready, 1)
                nc.vector.memset(pre[:, :, :, 0:TAPS - 1], 0.0).then_inc(pre_padded, 1)
                dve.wait_ge(pre_padded, 1)
                dve.wait_ge(conv_ready, 1)
                for k in range(3 * TAPS):
                    convolve(k, 0)
                with dve.Fori(0, STEPS - 1) as n:
                    step(n, True)
                step(STEPS - 1, False)

            @block.gpsimd
            def _(pool):
                def step(n):
                    pool.wait_ge(tok_ready, n + 1)
                    nc.gpsimd.tensor_tensor(g_cols[:, :, :], c.upper.unsqueeze(1).broadcast_to([P, U, P]),
                                            tok[:, G, :].unsqueeze(2).broadcast_to([P, U, P]), ALU.mult
                                            ).then_inc(g_cols_ready, 1)
                    pool.wait_ge(silu_done, 4 * n + 2)
                    nc.gpsimd.tensor_tensor(sq[:, :, :, :], qkv[:, 0:2, :, :], qkv[:, 0:2, :, :], ALU.mult
                                            ).then_inc(squared, 1)
                    pool.wait_ge(a_ready, U * n + U)
                    for level in range(1, NL):
                        if level == 3:
                            pool.wait_ge(norms_ready, n + 1)
                            pool.wait_ge(kv_copied, 2 * n + 1)
                            nc.gpsimd.tensor_tensor(v_tok[:, :, :], v_tok[:, :, :],
                                                    k_norm[:, :].unsqueeze(2).broadcast_to([P, U, P]), ALU.mult
                                                    ).then_inc(v_scaled, 1)
                        if level == 5:
                            pool.wait_ge(scores_read, n + 1)
                            nc.gpsimd.tensor_tensor(scores[:, :, :], scores[:, :, :],
                                                    c.upper.unsqueeze(1).broadcast_to([P, U, P]), ALU.mult
                                                    ).then_inc(scores_ready, 1)
                        if level > RING:
                            pool.wait_ge(y_done, 2 * (NL - 1) * n + 2 * (level - RING))
                        nc.gpsimd.tensor_tensor(a_level[:, level % RING, :, :], a_all[:, :, :],
                                                c.pair_mask(level).unsqueeze(1).broadcast_to([P, U, P]), ALU.mult
                                                ).then_inc(level_masked, 1)
                    pool.wait_ge(u_ready, 2 * n + 1)
                    nc.gpsimd.tensor_tensor(u_end[:, :, :], u[:, 0:HG, :],
                                            tok[:, TO_END, 0:HG].unsqueeze(2).broadcast_to([P, HG, P]), ALU.mult
                                            ).then_inc(u_end_ready, 1)

                with pool.Fori(0, STEPS) as n:
                    step(n)


def dense_stage(c, name, w_gate, w_up, w_down, scales=None):
    nc = c.nc
    FT = INTER // P
    W = 512
    steps = NT * P // W
    with ExitStack() as own:
        def sb(what, shape, dt=F32):
            return c.sb(f"{name}_{what}", shape, dt, ctx=own)

        def sem(what):
            return c.sem(f"{name}_{what}")

        up_sb = [sb("w_gate", [P, KD, INTER]), sb("w_up", [P, KD, INTER])]
        down_sb = sb("w_down", [P, FT, D])
        if scales:
            up_raw = [sb("w_gate_i8", [P, KD, INTER // 4], I32), sb("w_up_i8", [P, KD, INTER // 4], I32)]
            down_raw = sb("w_down_i8", [P, FT, D // 4], I32)
            s_cols = sb("s_cols", [P, 2, FT])
            s_row = sb("s_row", [1, D])
            s_down = sb("s_down", [P, D])
        gated = sb("gated", [P, 2, W])
        fused = sb("fused", [P, FT, W])
        scaled = sb("scaled", [P, W // P, D])
        loaded = sem("loaded")
        cast = sem("cast")
        s_spread = sem("s_spread")
        up_done = sem("up_done")
        silu_done = sem("silu_done")
        fused_done = sem("fused_done")
        down_done = sem("down_done")
        s_ready = sem("s_ready")
        out_scaled = sem("out_scaled")
        added = sem("added")
        with nc.Block() as block:
            @block.sync
            def _(sp):
                to = (up_raw + [down_raw]) if scales else (up_sb + [down_sb])
                for dst, src in zip(to, (w_gate, w_up, w_down)):
                    sp.dma_start(dst[:, :, :], src.rearrange("(k p) n -> p k n", p=P)).then_inc(loaded, 16)
                if scales:
                    with nc.allow_non_contiguous_dma("columns of 128 scales"):
                        for i in range(2):
                            sp.dma_start(s_cols[:, i, :], scales[i].rearrange("(k p) -> p k", p=P)
                                         ).then_inc(loaded, 16)
                    sp.dma_start(s_row[:, :], scales[2].rearrange("(a n) -> a n", a=1)).then_inc(loaded, 16)

            @block.gpsimd
            def _(pool):
                if scales:
                    pool.wait_ge(loaded, 96)
                    for dst, src in zip(up_sb, up_raw):
                        nc.gpsimd.tensor_copy(dst[:, :, :], src[:, :, :].bitcast(I8)).then_inc(cast, 1)
                    nc.gpsimd.tensor_copy(down_sb[:, :, :], down_raw[:, :, :].bitcast(I8)).then_inc(cast, 1)

            @block.tensor
            def _(pe):
                if scales:
                    pe.wait_ge(loaded, 96)
                    nc.tensor.matmul(c.psum[:, 7, 0:D], c.ones[0:1, :], s_row[:, :], start=True, stop=True
                                     ).then_inc(s_spread, 1)
                    pe.wait_ge(cast, 3)
                else:
                    pe.wait_ge(loaded, 48)
                with pe.Fori(0, steps) as g:
                    tokens = bass.ds(g * W, W)
                    for f in range(FT):
                        pe.wait_ge(fused_done, FT * g + f - 1 if f else FT * g)
                        for i in range(2):
                            for k in range(KD):
                                last = nc.tensor.matmul(c.psum[:, 2 * i + f % 2, :], up_sb[i][:, k, f * P:(f + 1) * P],
                                                        c.hT[:, k, tokens], start=k == 0, stop=k == KD - 1)
                            last.then_inc(up_done, 1)
                    pe.wait_ge(fused_done, FT * (g + 1))
                    pe.wait_ge(added, g)
                    for j in range(W // P):
                        for f in range(FT):
                            last = nc.tensor.matmul(c.psum[:, 4 + j // 2, (j % 2) * D:(j % 2 + 1) * D],
                                                    fused[:, f, j * P:(j + 1) * P], down_sb[:, f, :],
                                                    start=f == 0, stop=f == FT - 1)
                    last.then_inc(down_done, 1)

            @block.scalar
            def _(act):
                with act.Fori(0, steps) as g:
                    for f in range(FT):
                        act.wait_ge(up_done, 2 * FT * g + 2 * f + 1)
                        act.wait_ge(fused_done, FT * g + f - 1 if f else FT * g)
                        scale = s_cols[:, 0, f:f + 1] if scales else 1.0
                        nc.scalar.activation(gated[:, f % 2, :], c.psum[:, f % 2, :], ACT.Silu, scale=scale
                                             ).then_inc(silu_done, 1)

            @block.vector
            def _(dve):
                if scales:
                    dve.wait_ge(s_spread, 1)
                    nc.vector.tensor_copy(s_down[:, :], c.psum[:, 7, 0:D]).then_inc(s_ready, 1)
                    dve.wait_ge(s_ready, 1)
                with dve.Fori(0, steps) as g:
                    tiles = bass.ds(g * (W // P), W // P)
                    for f in range(FT):
                        dve.wait_ge(up_done, 2 * FT * g + 2 * f + 2)
                        dve.wait_ge(silu_done, FT * g + f + 1)
                        if f == 0:
                            dve.wait_ge(down_done, g)
                        up = c.psum[:, 2 + f % 2, :]
                        if scales:
                            op = nc.vector.scalar_tensor_tensor(fused[:, f, :], up, s_cols[:, 1, f:f + 1],
                                                                gated[:, f % 2, :], ALU.mult, ALU.mult)
                        else:
                            op = nc.vector.tensor_tensor(fused[:, f, :], up, gated[:, f % 2, :], ALU.mult)
                        op.then_inc(fused_done, 1)
                    dve.wait_ge(down_done, g + 1)
                    result = c.banks(4, 2, D)
                    if scales:
                        nc.vector.tensor_tensor(scaled[:, :, :], result,
                                                s_down[:, :].unsqueeze(1).broadcast_to([P, W // P, D]), ALU.mult
                                                ).then_inc(out_scaled, 1)
                        dve.wait_ge(out_scaled, g + 1)
                        result = scaled[:, :, :]
                    nc.vector.tensor_tensor(c.xs[:, tiles, :], c.xs[:, tiles, :], result, ALU.add).then_inc(added, 1)


def route_stage(c, io, gates_T):
    nc = c.nc
    with ExitStack() as own:
        def sb(what, shape):
            return c.sb("r_" + what, shape, ctx=own)

        def sem(what):
            return c.sem("r_" + what)

        cent = sb("cent", [NE, D])
        centT = sb("centT", [P, KD, NE])
        bias_row = sb("bias_row", [1, NE])
        bias = sb("bias", [P, NE])
        e = sb("e", [P, NT, NE])
        scores = sb("scores", [P, NT, NE])
        top = sb("top", [P, NT, 8])
        left = sb("left", [P, NT, NE])
        total = sb("total", [P, NT])
        loaded = sem("loaded")
        cent_turned = sem("cent_turned")
        cent_ready = sem("cent_ready")
        logits_done = sem("logits_done")
        exp_done = sem("exp_done")
        step = sem("step")
        gates_done = sem("gates_done")
        turned = sem("turned")
        ones_set = sem("ones_set")
        MANY = [P, NT, NE]
        with nc.Block() as block:
            @block.sync
            def _(sp):
                sp.dma_start(cent[:, :], io["L1_ffn_centroids"]).then_inc(loaded, 16)
                sp.dma_start(bias_row[:, :], io["L1_ffn_bias"].rearrange("(a n) -> a n", a=1)).then_inc(loaded, 16)

            @block.tensor
            def _(pe):
                pe.wait_ge(loaded, 32)
                for k in range(KD):
                    last = nc.tensor.transpose(c.psum[:, 0, k * NE:(k + 1) * NE], cent[:, k * P:(k + 1) * P],
                                               c.ident[0:NE, 0:NE])
                last.then_inc(cent_turned, 1)
                pe.wait_ge(cent_ready, 1)
                nc.tensor.matmul(c.psum[:, 1, 0:NE], c.ones[0:1, :], bias_row[:, :], start=True, stop=True)
                for n in range(NT):
                    for k in range(KD):
                        last = nc.tensor.matmul(c.psum[:, 2, n * NE:(n + 1) * NE], c.hT[:, k, n * P:(n + 1) * P],
                                                centT[:, k, :], start=k == 0, stop=k == KD - 1)
                last.then_inc(logits_done, 1)
                pe.wait_ge(gates_done, 1)
                for n in range(NT):
                    last = nc.tensor.transpose(c.psum[0:NE, 4 + n // 4, (n % 4) * P:(n % 4 + 1) * P],
                                               scores[:, n, :], c.ident)
                last.then_inc(turned, 1)

            @block.scalar
            def _(act):
                act.wait_ge(cent_turned, 1)
                nc.scalar.activation(centT[:, :, :], c.psum[:, 0, 0:KD * NE], ACT.Copy).then_inc(cent_ready, 1)
                act.wait_ge(logits_done, 1)
                nc.scalar.activation(e[:, :, :], c.psum[:, 2, 0:NT * NE], ACT.Exp, scale=-1.0).then_inc(exp_done, 1)
                act.wait_ge(turned, 1)
                act.wait_ge(ones_set, 1)
                nc.scalar.activation(gates_T[0:NE, :], c.psum[0:NE, 4:8, :].rearrange("p b n -> p (b n)"), ACT.Copy)

            @block.vector
            def _(dve):
                nc.vector.memset(gates_T[:, :], 1.0).then_inc(ones_set, 1)
                dve.wait_ge(exp_done, 1)
                nc.vector.tensor_copy(bias[:, :], c.psum[:, 1, 0:NE])
                nc.vector.tensor_scalar_add(e[:, :, :], e[:, :, :], 1.0).then_inc(step, 1)
                dve.wait_ge(step, 1)
                nc.vector.reciprocal(e[:, :, :], e[:, :, :]).then_inc(step, 1)
                dve.wait_ge(step, 2)
                nc.vector.tensor_tensor(scores[:, :, :], e[:, :, :], bias[:, :].unsqueeze(1).broadcast_to(MANY),
                                        ALU.add).then_inc(step, 1)
                dve.wait_ge(step, 3)
                for n in range(NT):
                    last = nc.vector.max(top[:, n, :], scores[:, n, :])
                last.then_inc(step, 1)
                dve.wait_ge(step, 4)
                nc.vector.memset(top[:, :, TOPK:8], 3.4e38).then_inc(step, 1)
                dve.wait_ge(step, 5)
                for n in range(NT):
                    last = nc.vector.match_replace(left[:, n, :], top[:, n, :], scores[:, n, :], 3.0e38)
                last.then_inc(step, 1)
                dve.wait_ge(step, 6)
                nc.vector.scalar_tensor_tensor(scores[:, :, :], left[:, :, :], 2.0e38, scores[:, :, :],
                                               ALU.is_gt, ALU.mult).then_inc(step, 1)
                dve.wait_ge(step, 7)
                nc.vector.tensor_reduce(total[:, :], scores[:, :, :], AX.X, ALU.add).then_inc(step, 1)
                dve.wait_ge(step, 8)
                nc.vector.tensor_scalar(total[:, :], total[:, :], 1e-8, None, ALU.max).then_inc(step, 1)
                dve.wait_ge(step, 9)
                nc.vector.reciprocal(total[:, :], total[:, :]).then_inc(step, 1)
                dve.wait_ge(step, 10)
                nc.vector.tensor_tensor(scores[:, :, :], scores[:, :, :],
                                        total[:, :].unsqueeze(2).broadcast_to(MANY), ALU.mult).then_inc(gates_done, 1)


def experts_stage(c, io, gates_T):
    nc = c.nc
    W = 512
    steps = NT * P // W
    shared_width = NS * DFF
    routed_width = NE * DFF
    tiles = [(True, f, min(P, shared_width - f)) for f in range(0, shared_width, P)]
    tiles += [(False, f, P) for f in range(0, routed_width, P)]
    FT = len(tiles)
    n_shared = FT - routed_width // P
    with ExitStack() as own:
        def sb(what, shape):
            return c.sb("e_" + what, shape, ctx=own)

        def sem(what):
            return c.sem("e_" + what)

        shared_w1 = sb("shared_w1", [P, KD, shared_width])
        routed_w1 = sb("routed_w1", [P, KD, routed_width])
        w2 = sb("w2", [P, FT, D])
        b1 = sb("b1", [P, FT])
        b2 = sb("b2", [NE + NS, D])
        expert = sb("expert", [NE, routed_width])
        gates = sb("gates", [NE + NS, W])
        relu = sb("relu", [P, 2, W])
        hidden = sb("hidden", [P, FT, W])
        loaded = sem("loaded")
        gates_ready = sem("gates_ready")
        up_done = sem("up_done")
        relu_done = sem("relu_done")
        hidden_done = sem("hidden_done")
        down_done = sem("down_done")
        added = sem("added")
        loads = 0
        with nc.Block() as block:
            @block.sync
            def _(sp):
                nonlocal loads

                def load(dst, src):
                    nonlocal loads
                    sp.dma_start(dst, src).then_inc(loaded, 16)
                    loads += 16

                for e in range(NS):
                    load(shared_w1[:, :, e * DFF:(e + 1) * DFF],
                         io["L1_ffn_shared_w1"][e].rearrange("(k p) f -> p k f", p=P))
                for k in range(KD):
                    load(routed_w1[:, k, :].rearrange("p (e f) -> p e f", f=DFF),
                         io["L1_ffn_routed_w1"][:, k * P:(k + 1) * P, :].rearrange("e p f -> p e f"))
                flat = io["L1_ffn_shared_w2"].rearrange("e f d -> (e f) d")
                whole = shared_width // P
                load(w2[:, 0:whole, :], flat[0:whole * P, :].rearrange("(a p) d -> p a d", p=P))
                load(w2[0:shared_width - whole * P, whole, :], flat[whole * P:, :])
                load(w2[:, n_shared:, :], io["L1_ffn_routed_w2"].rearrange("e f d -> (e f) d")
                     .rearrange("(a p) d -> p a d", p=P))
                load(b2[0:NE, :], io["L1_ffn_routed_b2"])
                load(b2[NE:, :], io["L1_ffn_shared_b2"])
                load(expert[:, :], io["expert_of_column"])
                flat = io["L1_ffn_shared_b1"].rearrange("e f -> (e f)")
                with nc.allow_non_contiguous_dma("columns of 128 biases"):
                    load(b1[:, 0:whole], flat[0:whole * P].rearrange("(a p) -> p a", p=P))
                    load(b1[0:shared_width - whole * P, whole:whole + 1], flat[whole * P:].rearrange("(p a) -> p a", a=1))
                    load(b1[:, n_shared:], io["L1_ffn_routed_b1"].rearrange("e f -> (e f)")
                         .rearrange("(a p) -> p a", p=P))

            @block.tensor
            def _(pe):
                pe.wait_ge(loaded, loads)
                with pe.Fori(0, steps) as g:
                    pe.wait_ge(gates_ready, g + 1)
                    for n, (shared, f, m) in enumerate(tiles):
                        pe.wait_ge(hidden_done, FT * g + n - 1 if n else FT * g)
                        w1 = shared_w1 if shared else routed_w1
                        for k in range(KD):
                            last = nc.tensor.matmul(c.psum[0:m, n % 2, :], w1[:, k, f:f + m],
                                                    c.hT[:, k, bass.ds(g * W, W)], start=k == 0, stop=k == KD - 1)
                        if not shared:
                            last = nc.tensor.matmul(c.psum[:, 2 + n % 2, :], expert[:, f:f + P], gates[0:NE, :],
                                                    start=True, stop=True)
                        last.then_inc(up_done, 1)
                    pe.wait_ge(hidden_done, FT * (g + 1))
                    pe.wait_ge(added, g)
                    for j in range(W // P):
                        out = c.psum[:, 4 + j // 2, (j % 2) * D:(j % 2 + 1) * D]
                        for n, (shared, f, m) in enumerate(tiles):
                            nc.tensor.matmul(out, hidden[0:m, n, j * P:(j + 1) * P], w2[0:m, n, :],
                                             start=n == 0, stop=False)
                        last = nc.tensor.matmul(out, gates[:, j * P:(j + 1) * P], b2[:, :], start=False, stop=True)
                    last.then_inc(down_done, 1)

            @block.scalar
            def _(act):
                act.wait_ge(loaded, loads)
                with act.Fori(0, steps) as g:
                    for n, (shared, f, m) in enumerate(tiles):
                        act.wait_ge(up_done, FT * g + n + 1)
                        act.wait_ge(hidden_done, FT * g + n - 1 if n else FT * g)
                        if shared and n == 0:
                            act.wait_ge(down_done, g)
                        to = hidden[0:m, n, :] if shared else relu[0:m, n % 2, :]
                        op = nc.scalar.activation(to, c.psum[0:m, n % 2, :], ACT.Relu, bias=b1[0:m, n:n + 1])
                        op.then_inc(relu_done, 1)

            @block.vector
            def _(dve):
                with dve.Fori(0, steps) as g:
                    dve.wait_ge(down_done, g)
                    nc.vector.tensor_scalar(gates[:, :], gates_T[:, bass.ds(g * W, W)], 1.0, None, ALU.mult
                                            ).then_inc(gates_ready, 1)
                    for n, (shared, f, m) in enumerate(tiles):
                        dve.wait_ge(relu_done, FT * g + n + 1)
                        if shared:
                            dve.sem_inc(hidden_done, 1)
                        else:
                            nc.vector.tensor_tensor(hidden[:, n, :], c.psum[:, 2 + n % 2, :], relu[:, n % 2, :], ALU.mult
                                                    ).then_inc(hidden_done, 1)
                    dve.wait_ge(down_done, g + 1)
                    rows = c.xs[:, bass.ds(g * (W // P), W // P), :]
                    nc.vector.tensor_tensor(rows, rows, c.banks(4, 2, D), ALU.add).then_inc(added, 1)


def slots_stages(c, io):
    with ExitStack() as own:
        f_T = c.sb("f_T1", [P, NT * P], ctx=own)
        gate_T = c.sb("gate_T1", [P, NT * P], ctx=own)
        beta = c.sb("beta1", [P, NG, B, U], ctx=own)
        narrow_stage(c, "n1b", io["L1_attn_Wf1"], io["L1_attn_Wg1"], io["L1_attn_Wb"], f_T, gate_T, beta)
        slots_stage(c, io, f_T, gate_T, beta)


def slots_stage(c, io, f_T, gate_T, beta):
    nc = c.nc
    Q, K, V, W = range(4)
    TAPS = 4
    HALF = P // 2
    EPS = 1e-5
    RING = 3
    with ExitStack() as own:
        def sb(name, shape):
            return c.sb("s_" + name, shape, ctx=own)

        def sem(name):
            return c.sem("s_" + name)

        conv_all = sb("conv_all", [P, 3, H, TAPS])
        conv = sb("conv", [P, 3, HG, TAPS])
        norm_w = sb("norm_w", [P, 1])
        bias_rows = sb("bias_rows", [H, P])
        bias_all = sb("bias_all", [P, H])
        bias = sb("bias", [P, HG])
        w_in = sb("w_in", [P, 4, KD, HG * P])
        w_decay = sb("w_decay", [P, HG * P])
        w_gate = sb("w_gate", [P, HG * P])
        w_o = sb("w_o", [P, HG, D])
        f = sb("f", [P, T])
        beta_now = sb("beta_now", [P, U])
        pre = sb("pre", [P, 2, HG, T + TAPS - 1])
        act_in = sb("act_in", [P, 4, HG, T])
        sq = sb("sq", [P, HG, T])
        bw_tok = sb("bw_tok", [P, U, P])
        bwT = sb("bwT", [P, U, P])
        v_tok = sb("v_tok", [P, U, P])
        k_tok = sb("k_tok", [P, HG, P])
        g_tok = sb("g_tok", [P, U, P])
        g_temp = sb("g_temp", [P, U, P])
        pairs = sb("pairs", [P, U, P])
        pairs_level = sb("pairs_level", [P, 2, U, HALF])
        uj = sb("uj", [P, RING, U, P])
        mid_high = sb("mid_high", [P, NL - 4, U, P])
        y_scaled = sb("y_scaled", [P, U, HALF])
        decay_end = sb("decay_end", [P, HG, P])
        start_T = sb("start_T", [P, HG, P])
        a_start_T = sb("a_start_T", [P, HG, P])
        state_k = sb("state_k", [P, HG, P])
        state_v = sb("state_v", [P, HG, P])
        gate = sb("gate", [P, HG, T])
        sums = sb("sums", [P, U])
        w_scale = sb("w_scale", [P, U])
        top = sb("top", [P, U])
        total = sb("total", [P, U])
        o_sums = sb("o_sums", [P, U])
        o_scale = sb("o_scale", [P, U])

        x_place = c.x[:, :, :].rearrange("p n d -> p (n d)").rearrange("p (l u m) -> p l u m", l=4, u=U)
        sT = act_in[:, V, :, :].rearrange("p h t -> p (h t)").rearrange("p (u m) -> p u m", u=U)
        a = act_in[:, W, :, :].rearrange("p h t -> p (h t)").rearrange("p (u m) -> p u m", u=U)
        o = act_in[:, K, :, :].rearrange("p h t -> p (h t)").rearrange("p (u m) -> p u m", u=U)
        aT = sq[:, :, :].rearrange("p h t -> p (h t)").rearrange("p (u m) -> p u m", u=U)
        mix = g_temp
        oT = pairs

        def mid_T(level):
            return x_place[:, level] if level < 4 else mid_high[:, level - 4]

        def halves(v, level, right):
            return v.rearrange("p u (b two s) -> p u b two s", two=2, s=1 << level)[:, :, :, right, :]

        def halves2(v, level, right):
            return v.rearrange("p (b two s) -> p b two s", two=2, s=1 << level)[:, :, right, :]

        def packed(v, level):
            return v.rearrange("p u (b s) -> p u b s", s=1 << level)

        def spread(v, level):
            return v.unsqueeze(1).broadcast_to([P, U, P >> (level + 1), 1 << level])

        def bank_of(unit, first):
            return c.psum[:, first + unit // HG, (unit % HG) * P:(unit % HG + 1) * P]

        def half_bank(unit, bank):
            return c.psum[:, bank, unit * HALF:(unit + 1) * HALF]

        def half_banks(bank):
            return c.psum[:, bank, :].rearrange("p (u n) -> p u n", u=U)

        def chunk(w, unit):
            return act_in[:, w, unit % HG, (unit // HG) * P:(unit // HG + 1) * P]

        consts_in = sem("consts_in")
        bias_turned = sem("bias_turned")
        bias_ready = sem("bias_ready")
        weights_in = sem("weights_in")
        now_ready = sem("now_ready")
        projected = sem("projected")
        pre_ready = sem("pre_ready")
        conv_step = sem("conv_step")
        silu_done = sem("silu_done")
        g_lin_done = sem("g_lin_done")
        g_abs = sem("g_abs")
        g_log = sem("g_log")
        g_ready = sem("g_ready")
        squared = sem("squared")
        v_turned = sem("v_turned")
        k_turned = sem("k_turned")
        w_turned = sem("w_turned")
        v_ready = sem("v_ready")
        k_ready = sem("k_ready")
        sq_summed = sem("sq_summed")
        eps_added = sem("eps_added")
        log_done = sem("log_done")
        w_rnorm = sem("w_rnorm")
        w_scale_ready = sem("w_scale_ready")
        bw_ready = sem("bw_ready")
        bw_turned = sem("bw_turned")
        bwT_ready = sem("bwT_ready")
        pairs_done = sem("pairs_done")
        pairs_ready = sem("pairs_ready")
        own_pairs = sem("own_pairs")
        own_done = sem("own_done")
        sT_begun = sem("sT_begun")
        mid_summed = sem("mid_summed")
        midT_summed = sem("midT_summed")
        mid_ready = sem("mid_ready")
        midT_ready = sem("midT_ready")
        level_ready = sem("level_ready")
        left_ready = sem("left_ready")
        y_done = sem("y_done")
        y_scaled_done = sem("y_scaled_done")
        y_added = sem("y_added")
        end_ready = sem("end_ready")
        state_done = sem("state_done")
        state_ready = sem("state_ready")
        s_state_done = sem("s_state_done")
        s_scaled = sem("s_scaled")
        sT_ready = sem("sT_ready")
        s_turned = sem("s_turned")
        max_done = sem("max_done")
        top_ready = sem("top_ready")
        a_ready = sem("a_ready")
        a_turned = sem("a_turned")
        aT_ready = sem("aT_ready")
        a_start_ready = sem("a_start_ready")
        total_ready = sem("total_ready")
        right_ready = sem("right_ready")
        own_mix_done = sem("own_mix_done")
        mix_begun = sem("mix_begun")
        mix_done = sem("mix_done")
        mix_kept = sem("mix_kept")
        o_done = sem("o_done")
        gate_done = sem("gate_done")
        o_squared = sem("o_squared")
        o_eps = sem("o_eps")
        o_log = sem("o_log")
        o_rstd = sem("o_rstd")
        o_scale_ready = sem("o_scale_ready")
        o_normed = sem("o_normed")
        o_turned = sem("o_turned")
        gate_ready = sem("gate_ready")
        o_gated = sem("o_gated")
        out_done = sem("out_done")
        added = sem("added")

        with nc.Block() as block:
            @block.sync
            def _(sp):
                for i, name in enumerate(("cq", "ck", "cv")):
                    sp.dma_start(conv_all[:, i, :, :], io["L1_attn_" + name].rearrange("(h p) a -> p h a", p=P)
                                 ).then_inc(consts_in, 16)
                sp.dma_start(norm_w[:, :], io["L1_attn_norm_w"].rearrange("(p a) -> p a", a=1)).then_inc(consts_in, 16)
                sp.dma_start(bias_rows[:, :], io["L1_attn_bg2"].rearrange("(h p) -> h p", p=P)).then_inc(consts_in, 16)
                with sp.Fori(0, NG) as hg:
                    sp.wait_ge(out_done, B * hg)
                    heads = bass.ds(hg * (HG * P), HG * P)
                    for w, name in enumerate(("Wq", "Wk", "Wv", "Ww")):
                        sp.dma_start(w_in[:, w, :, :], io["L1_attn_" + name].rearrange("(k p) n -> p k n", p=P)[:, :, heads]
                                     ).then_inc(weights_in, 16)
                    sp.dma_start(w_decay[:, :], io["L1_attn_Wf2"][:, heads]).then_inc(weights_in, 16)
                    sp.dma_start(w_gate[:, :], io["L1_attn_Wg2"][:, heads]).then_inc(weights_in, 16)
                    sp.dma_start(w_o[:, :, :], io["L1_attn_Wo"].rearrange("(g h p) n -> p g h n", p=P, h=HG)
                                 [:, bass.ds(hg, 1), :, :]).then_inc(weights_in, 16)

            @block.tensor
            def _(pe):
                pe.wait_ge(consts_in, 80)
                nc.tensor.transpose(c.psum[:, 0, 0:H], bias_rows[:, :], c.ident[0:H, 0:H]).then_inc(bias_turned, 1)
                pe.wait_ge(bias_ready, 1)
                with pe.Fori(0, NG) as hg:
                    with pe.Fori(0, B) as seq:
                        n = hg * B + seq
                        pe.wait_ge(weights_in, 112 * (hg + 1))
                        pe.wait_ge(added, n)
                        for w in range(4):
                            for h in range(HG):
                                for k in range(KD):
                                    last = nc.tensor.matmul(
                                        c.psum[:, 2 * w + h // 2, (h % 2) * T:(h % 2 + 1) * T],
                                        w_in[:, w, k, h * P:(h + 1) * P], c.hT[:, k, bass.ds(seq * T, T)],
                                        start=k == 0, stop=k == KD - 1)
                            last.then_inc(projected, 1)
                        pe.wait_ge(pre_ready, 4 * n + 1)
                        pe.wait_ge(now_ready, n + 2)
                        for half in range(2):
                            last = nc.tensor.matmul(c.psum[:, half, :], f[:, half * P:(half + 1) * P], w_decay[:, :],
                                                    start=True, stop=True)
                        last.then_inc(g_lin_done, 1)
                        pe.wait_ge(silu_done, 4 * n + 4)
                        for i in range(U):
                            last = nc.tensor.transpose(bank_of(i, 2), chunk(V, i), c.ident)
                        last.then_inc(v_turned, 1)
                        for i in range(HG):
                            last = nc.tensor.transpose(bank_of(i, 4), chunk(K, i), c.ident)
                        last.then_inc(k_turned, 1)
                        for i in range(U):
                            last = nc.tensor.transpose(bank_of(i, 5), chunk(W, i), c.ident)
                        last.then_inc(w_turned, 1)
                        pe.wait_ge(squared, n + 1)
                        for i in range(U):
                            last = nc.tensor.matmul(c.psum[:, 7, i:i + 1],
                                                    sq[:, i % HG, (i // HG) * P:(i // HG + 1) * P],
                                                    c.ones[:, 0:1], start=True, stop=True)
                        last.then_inc(sq_summed, 1)
                        pe.wait_ge(g_ready, n + 1)
                        for i in range(U):
                            last = nc.tensor.matmul(bank_of(i, 0), chunk(K, i), chunk(Q, i), start=True, stop=True)
                        last.then_inc(pairs_done, 1)
                        pe.wait_ge(v_ready, n + 1)
                        pe.wait_ge(bw_ready, n + 1)
                        for i in range(U):
                            last = nc.tensor.transpose(bank_of(i, 2), bw_tok[:, i, :], c.ident)
                        last.then_inc(bw_turned, 1)
                        for level in range(NL + 3):
                            if level < NL:
                                if level:
                                    pe.wait_ge(mid_ready, NL * n + level)
                                for half in range(2):
                                    last = nc.tensor.matmul(c.psum[:, 4 + half, :], c.level_sums(level),
                                                            g_tok[:, half * HG:(half + 1) * HG, :],
                                                            start=True, stop=True)
                                last.then_inc(mid_summed, 1)
                                if level:
                                    pe.wait_ge(midT_ready, NL * n + level)
                                for i in range(U):
                                    last = nc.tensor.matmul(bank_of(i, 6), g_tok[:, i, :], c.level_sums(level),
                                                            start=True, stop=True)
                                last.then_inc(midT_summed, 1)
                            if level == 0:
                                pe.wait_ge(bwT_ready, n + 1)
                                pe.wait_ge(own_pairs, n + 1)
                                for i in range(U):
                                    last = nc.tensor.matmul(bank_of(i, 2), bw_tok[:, i, :], uj[:, RING - 1, i, :],
                                                            start=True, stop=True)
                                last.then_inc(own_done, 1)
                            if 2 <= level < NL + 2:
                                l = level - 2
                                pe.wait_ge(level_ready, NL * n + l + 1)
                                if l >= 2:
                                    pe.wait_ge(y_scaled_done, NL * n + l - 1)
                                for i in range(U):
                                    last = nc.tensor.matmul(half_bank(i, l % 2), uj[:, l % RING, i, :],
                                                            pairs_level[:, l % 2, i, :], start=True, stop=True)
                                last.then_inc(y_done, 1)
                            if level == NL:
                                pe.wait_ge(mid_ready, NL * (n + 1))
                                nc.tensor.matmul(c.psum[:, 4, :], c.lower, g_tok[:, 0:HG, :],
                                                 start=True, stop=True).then_inc(mid_summed, 1)
                                pe.wait_ge(midT_ready, NL * (n + 1))
                                for i in range(HG):
                                    last = nc.tensor.matmul(bank_of(i, 6), g_tok[:, HG + i, :], c.upper,
                                                            start=True, stop=True)
                                last.then_inc(midT_summed, 1)
                        pe.wait_ge(sT_begun, n + 1)
                        pe.wait_ge(end_ready, 3 * n + 3)
                        for i in range(HG):
                            last = nc.tensor.matmul(bank_of(i, 2), k_tok[:, i, :], decay_end[:, i, :],
                                                    start=True, stop=True)
                        last.then_inc(state_done, 1)
                        for i in range(HG):
                            last = nc.tensor.matmul(bank_of(i, 3), decay_end[:, i, :], v_tok[:, i, :],
                                                    start=True, stop=True)
                        last.then_inc(state_done, 1)
                        pe.wait_ge(state_ready, 2 * n + 1)
                        for i in range(HG):
                            last = nc.tensor.matmul(bank_of(i, 2), state_k[:, i, :], chunk(Q, HG + i),
                                                    start=True, stop=True)
                        last.then_inc(s_state_done, 1)
                        pe.wait_ge(sT_ready, n + 1)
                        for i in range(U):
                            last = nc.tensor.transpose(bank_of(i, 4), sT[:, i, :], c.ident)
                        last.then_inc(s_turned, 1)
                        pe.wait_ge(a_ready, n + 1)
                        for i in range(U):
                            last = nc.tensor.transpose(bank_of(i, 6), a[:, i, :], c.ident)
                        last.then_inc(a_turned, 1)
                        pe.wait_ge(aT_ready, n + 1)
                        pe.wait_ge(state_ready, 2 * n + 2)
                        for i in range(U):
                            last = nc.tensor.matmul(bank_of(i, 2), bwT[:, i, :], aT[:, i, :], start=True, stop=True)
                        last.then_inc(own_mix_done, 1)
                        for l in range(NL):
                            pe.wait_ge(left_ready, NL * n + l + 1)
                            pe.wait_ge(right_ready, NL * n + l + 1)
                            if l >= 2:
                                pe.wait_ge(mix_kept, NL * n + l - 1)
                            for i in range(U):
                                last = nc.tensor.matmul(half_bank(i, l % 2), mid_T(l)[:, i, :],
                                                        halves(mid_T(l), l, 1)[:, i, :, :], start=True, stop=True)
                            last.then_inc(mix_done, 1)
                        pe.wait_ge(mix_begun, n + 1)
                        for h in range(HG):
                            last = nc.tensor.matmul(c.psum[:, 2 + h // 2, (h % 2) * T:(h % 2 + 1) * T],
                                                    w_gate[:, h * P:(h + 1) * P], gate_T[:, bass.ds(seq * T, T)],
                                                    start=True, stop=True)
                        last.then_inc(gate_done, 1)
                        pe.wait_ge(mix_kept, NL * (n + 1))
                        pe.wait_ge(a_start_ready, n + 1)
                        for i in range(U):
                            last = nc.tensor.matmul(bank_of(i, 4), mix[:, i, :], v_tok[:, i, :],
                                                    start=True, stop=i < HG)
                            if i >= HG:
                                last = nc.tensor.matmul(bank_of(i, 4), a_start_T[:, i - HG, :], state_v[:, i - HG, :],
                                                        start=False, stop=True)
                        last.then_inc(o_done, 1)
                        pe.wait_ge(o_normed, n + 1)
                        for i in range(U):
                            last = nc.tensor.transpose(bank_of(i, 6), o[:, i, :], c.ident)
                        last.then_inc(o_turned, 1)
                        pe.wait_ge(o_gated, n + 1)
                        for half in range(2):
                            for h in range(HG):
                                last = nc.tensor.matmul(c.psum[:, 0, half * D:(half + 1) * D], oT[:, half * HG + h, :],
                                                        w_o[:, h, :], start=h == 0, stop=h == HG - 1)
                        last.then_inc(out_done, 1)

            @block.scalar
            def _(act):
                act.wait_ge(bias_turned, 1)
                nc.scalar.activation(bias_all[:, :], c.psum[:, 0, 0:H], ACT.Copy).then_inc(bias_ready, 1)
                with act.Fori(0, NG) as hg:
                    with act.Fori(0, B) as seq:
                        n = hg * B + seq

                        def silu(w):
                            act.wait_ge(conv_step, 64 * n + 16 * (w + 1))
                            nc.scalar.activation(act_in[:, w, :, :], act_in[:, w, :, :], ACT.Silu).then_inc(silu_done, 1)

                        for w in range(4):
                            if w >= 2:
                                silu(w - 2)
                            act.wait_ge(projected, 4 * n + w + 1)
                            nc.scalar.activation(pre[:, w % 2, :, TAPS - 1:], c.banks(2 * w, 2, T), ACT.Copy
                                                 ).then_inc(pre_ready, 1)
                        silu(2)
                        silu(3)
                        nc.scalar.preload_act_table_set(EXP_LN)
                        act.wait_ge(g_lin_done, n + 1)
                        nc.scalar.activation(g_temp[:, :, :], c.banks(0, 2, P), ACT.Abs).then_inc(g_abs, 1)
                        act.wait_ge(g_abs, 2 * n + 1)
                        nc.scalar.activation(g_temp[:, :, :], g_temp[:, :, :], ACT.Exp, scale=-1.0).then_inc(g_abs, 1)
                        act.wait_ge(g_abs, 2 * n + 2)
                        nc.scalar.activation(g_temp[:, :, :], g_temp[:, :, :], ACT.Ln, bias=1.0).then_inc(g_log, 1)
                        act.wait_ge(v_turned, n + 1)
                        nc.scalar.activation(v_tok[:, :, :], c.banks(2, 2, P), ACT.Copy).then_inc(v_ready, 1)
                        act.wait_ge(k_turned, n + 1)
                        nc.scalar.activation(k_tok[:, :, :], c.banks(4, 1, P), ACT.Copy).then_inc(k_ready, 1)
                        act.wait_ge(eps_added, n + 1)
                        nc.scalar.activation(sums[:, :], sums[:, :], ACT.Ln).then_inc(log_done, 1)
                        act.wait_ge(log_done, n + 1)
                        nc.scalar.activation(sums[:, :], sums[:, :], ACT.Exp, scale=-0.5).then_inc(w_rnorm, 1)
                        act.wait_ge(w_scale_ready, n + 1)
                        for i in range(U):
                            last = nc.scalar.activation(bw_tok[:, i, :], bank_of(i, 5), ACT.Copy, scale=w_scale[:, i:i + 1])
                        last.then_inc(bw_ready, 1)
                        act.wait_ge(pairs_done, n + 1)
                        nc.scalar.activation(pairs[:, :, :], c.banks(0, 2, P), ACT.Copy).then_inc(pairs_ready, 1)
                        act.wait_ge(bw_turned, n + 1)
                        nc.scalar.activation(bwT[:, :, :], c.banks(2, 2, P), ACT.Copy).then_inc(bwT_ready, 1)
                        for level in range(NL):
                            act.wait_ge(mid_summed, (NL + 1) * n + level + 1)
                            if level == RING - 1:
                                act.wait_ge(own_done, n + 1)
                            if level >= RING:
                                act.wait_ge(y_done, NL * n + level - RING + 1)
                            nc.scalar.activation(uj[:, level % RING, :, :], c.banks(4, 2, P), ACT.Exp).then_inc(mid_ready, 1)
                            act.wait_ge(midT_summed, (NL + 1) * n + level + 1)
                            nc.scalar.activation(mid_T(level), c.banks(6, 2, P), ACT.Exp).then_inc(midT_ready, 1)
                        act.wait_ge(mid_summed, (NL + 1) * (n + 1))
                        nc.scalar.activation(decay_end[:, :, :], c.banks(4, 1, P), ACT.Exp).then_inc(end_ready, 1)
                        act.wait_ge(midT_summed, (NL + 1) * (n + 1))
                        nc.scalar.activation(start_T[:, :, :], c.banks(6, 1, P), ACT.Exp).then_inc(end_ready, 1)
                        act.wait_ge(state_done, 2 * n + 1)
                        nc.scalar.activation(state_k[:, :, :], c.banks(2, 1, P), ACT.Copy).then_inc(state_ready, 1)
                        act.wait_ge(state_done, 2 * n + 2)
                        nc.scalar.activation(state_v[:, :, :], c.banks(3, 1, P), ACT.Copy).then_inc(state_ready, 1)
                        act.wait_ge(top_ready, n + 1)
                        for i in range(U):
                            last = nc.scalar.activation(a[:, i, :], bank_of(i, 4), ACT.Exp, bias=top[:, i:i + 1],
                                                        scale=SCALE, accum_out=total[:, i:i + 1])
                        last.then_inc(a_ready, 1)
                        act.wait_ge(a_turned, n + 1)
                        nc.scalar.activation(aT, c.banks(6, 2, P), ACT.Copy).then_inc(aT_ready, 1)
                        act.wait_ge(total_ready, n + 1)
                        act.wait_ge(o_done, n + 1)
                        for i in range(U):
                            last = nc.scalar.activation(uj[:, 0, i, :], bank_of(i, 4), ACT.Square,
                                                        scale=total[:, i:i + 1], accum_out=o_sums[:, i:i + 1])
                        last.then_inc(o_squared, 1)
                        act.wait_ge(o_eps, n + 1)
                        nc.scalar.activation(o_sums[:, :], o_sums[:, :], ACT.Ln).then_inc(o_log, 1)
                        act.wait_ge(o_log, n + 1)
                        nc.scalar.activation(o_sums[:, :], o_sums[:, :], ACT.Exp, scale=-0.5).then_inc(o_rstd, 1)
                        act.wait_ge(o_scale_ready, n + 1)
                        for i in range(U):
                            last = nc.scalar.activation(o[:, i, :], bank_of(i, 4), ACT.Copy, scale=o_scale[:, i:i + 1])
                        last.then_inc(o_normed, 1)
                        act.wait_ge(gate_done, n + 1)
                        for h in range(HG):
                            last = nc.scalar.activation(gate[:, h, :],
                                                        c.psum[:, 2 + h // 2, (h % 2) * T:(h % 2 + 1) * T],
                                                        ACT.Sigmoid, bias=bias[:, h:h + 1])
                        last.then_inc(gate_ready, 1)

            @block.vector
            def _(dve):
                nc.vector.memset(pre[:, :, :, 0:TAPS - 1], 0.0).then_inc(now_ready, 1)
                dve.wait_ge(bias_ready, 1)
                with dve.Fori(0, NG) as hg:
                    with dve.Fori(0, B) as seq:
                        n = hg * B + seq
                        heads = bass.ds(hg * HG, HG)
                        nc.vector.tensor_copy(conv[:, :, :, :], conv_all[:, :, heads, :])
                        nc.vector.tensor_copy(bias[:, :], bias_all[:, heads])
                        nc.vector.tensor_copy(beta_now[:, :],
                                              beta.rearrange("p g b u -> p (g b) u")[:, bass.ds(n, 1), :])
                        nc.vector.tensor_copy(f[:, :], f_T[:, bass.ds(seq * T, T)]).then_inc(now_ready, 1)
                        dve.wait_ge(now_ready, n + 2)
                        for w in range(4):
                            dve.wait_ge(pre_ready, 4 * n + w + 1)
                            for step, tap in enumerate(range(TAPS - 1, -1, -1)):
                                if step:
                                    dve.wait_ge(conv_step, 64 * n + 16 * w + 4 * step)
                                for h in range(HG):
                                    source = pre[:, w % 2, h, tap:tap + T]
                                    weight = conv[:, min(w, V), h, tap:tap + 1]
                                    if step == 0:
                                        op = nc.vector.tensor_scalar(act_in[:, w, h, :], source, weight, None, ALU.mult)
                                    else:
                                        op = nc.vector.scalar_tensor_tensor(act_in[:, w, h, :], source, weight,
                                                                            act_in[:, w, h, :], ALU.mult, ALU.add)
                                    op.then_inc(conv_step, 1)
                        dve.wait_ge(g_log, n + 1)
                        nc.vector.scalar_tensor_tensor(g_tok[:, :, :], c.banks(0, 2, P), 0.0, g_temp[:, :, :],
                                                       ALU.min, ALU.subtract).then_inc(g_ready, 1)
                        dve.wait_ge(sq_summed, n + 1)
                        nc.vector.tensor_scalar_add(sums[:, :], c.psum[:, 7, 0:U], 1e-6).then_inc(eps_added, 1)
                        dve.wait_ge(w_rnorm, n + 1)
                        nc.vector.tensor_tensor(w_scale[:, :], sums[:, :], beta_now[:, :], ALU.mult
                                                ).then_inc(w_scale_ready, 1)
                        dve.wait_ge(own_done, n + 1)
                        nc.vector.tensor_copy(sT, c.banks(2, 2, P)).then_inc(sT_begun, 1)
                        dve.wait_ge(sT_begun, n + 1)
                        for l in range(NL):
                            dve.wait_ge(y_done, NL * n + l + 1)
                            dve.wait_ge(midT_ready, NL * n + l + 1)
                            if l:
                                dve.wait_ge(y_added, NL * n + l)
                            nc.vector.tensor_tensor(packed(y_scaled[:, :, :], l), packed(half_banks(l % 2), l),
                                                    halves(mid_T(l), l, 1), ALU.mult).then_inc(y_scaled_done, 1)
                            dve.wait_ge(y_scaled_done, NL * n + l + 1)
                            nc.vector.tensor_tensor(halves(sT, l, 1), halves(sT, l, 1), packed(y_scaled[:, :, :], l),
                                                    ALU.add).then_inc(y_added, 1)
                        dve.wait_ge(s_state_done, n + 1)
                        dve.wait_ge(y_added, NL * (n + 1))
                        from_state = y_scaled[:, :, :].rearrange("p u n -> p (u n)").rearrange("p (h n) -> p h n", n=P)
                        nc.vector.tensor_tensor(from_state, c.banks(2, 1, P), start_T[:, :, :], ALU.mult
                                                ).then_inc(s_scaled, 1)
                        dve.wait_ge(s_scaled, n + 1)
                        nc.vector.tensor_tensor(sT[:, HG:U, :], sT[:, HG:U, :], from_state, ALU.add).then_inc(sT_ready, 1)
                        dve.wait_ge(s_turned, n + 1)
                        nc.vector.tensor_reduce(top[:, :], c.banks(4, 2, P), AX.X, ALU.max).then_inc(max_done, 1)
                        dve.wait_ge(max_done, n + 1)
                        nc.vector.tensor_scalar(top[:, :], top[:, :], -SCALE, None, ALU.mult).then_inc(top_ready, 1)

                        def right(l):
                            nc.vector.tensor_tensor(halves(mid_T(l), l, 1), halves(mid_T(l), l, 1), halves(aT, l, 1),
                                                    ALU.mult).then_inc(right_ready, 1)

                        dve.wait_ge(aT_ready, n + 1)
                        right(0)
                        right(1)
                        dve.wait_ge(own_mix_done, n + 1)
                        nc.vector.tensor_tensor(mix[:, :, :], c.banks(2, 2, P),
                                                c.ident.unsqueeze(1).broadcast_to([P, U, P]), ALU.mult
                                                ).then_inc(mix_begun, 1)
                        for l in range(NL):
                            dve.wait_ge(mix_done, NL * n + l + 1)
                            if l:
                                dve.wait_ge(mix_kept, NL * n + l)
                            else:
                                dve.wait_ge(mix_begun, n + 1)
                            if l + 2 < NL:
                                right(l + 2)
                            elif l == NL - 2:
                                nc.vector.tensor_tensor(a_start_T[:, :, :], aT[:, HG:U, :], start_T[:, :, :], ALU.mult
                                                        ).then_inc(a_start_ready, 1)
                            else:
                                nc.vector.reciprocal(total[:, :], total[:, :]).then_inc(total_ready, 1)
                            nc.vector.copy_predicated(halves(mix[:, :, :], l, 1),
                                                      spread(halves2(c.pair_mask(l), l, 1), l).bitcast(U32),
                                                      packed(half_banks(l % 2), l)).then_inc(mix_kept, 1)
                        dve.wait_ge(o_squared, n + 1)
                        nc.vector.tensor_scalar(o_sums[:, :], o_sums[:, :], 1.0 / P, EPS, ALU.mult, ALU.add
                                                ).then_inc(o_eps, 1)
                        dve.wait_ge(o_rstd, n + 1)
                        nc.vector.tensor_tensor(o_scale[:, :], o_sums[:, :], total[:, :], ALU.mult
                                                ).then_inc(o_scale_ready, 1)
                        dve.wait_ge(o_turned, n + 1)
                        dve.wait_ge(gate_ready, n + 1)
                        for half in range(2):
                            last = nc.vector.scalar_tensor_tensor(oT[:, half * HG:(half + 1) * HG, :],
                                                                  c.banks(6 + half, 1, P), norm_w[:, 0:1],
                                                                  gate[:, :, half * P:(half + 1) * P],
                                                                  ALU.mult, ALU.mult)
                        last.then_inc(o_gated, 1)
                        dve.wait_ge(out_done, n + 1)
                        nc.vector.tensor_tensor(c.xs[:, bass.ds(2 * seq, 2), :], c.xs[:, bass.ds(2 * seq, 2), :],
                                                c.banks(0, 1, D), ALU.add).then_inc(added, 1)

            @block.gpsimd
            def _(pool):
                with pool.Fori(0, NG) as hg:
                    with pool.Fori(0, B) as seq:
                        n = hg * B + seq
                        pool.wait_ge(silu_done, 4 * n + 4)
                        nc.gpsimd.tensor_tensor(sq[:, :, :], act_in[:, W, :, :], act_in[:, W, :, :], ALU.mult
                                                ).then_inc(squared, 1)
                        pool.wait_ge(pairs_ready, n + 1)
                        nc.gpsimd.tensor_tensor(uj[:, RING - 1, :, :], pairs[:, :, :],
                                                c.ident.unsqueeze(1).broadcast_to([P, U, P]), ALU.mult
                                                ).then_inc(own_pairs, 1)
                        for l in range(NL):
                            if l >= 2:
                                pool.wait_ge(y_done, NL * n + l - 1)
                            nc.gpsimd.tensor_tensor(packed(pairs_level[:, l % 2, :, :], l),
                                                    halves(pairs[:, :, :], l, 1),
                                                    spread(halves2(c.pair_mask(l), l, 1), l), ALU.mult)
                            pool.wait_ge(mid_ready, NL * n + l + 1)
                            nc.gpsimd.tensor_tensor(uj[:, l % RING, :, :], uj[:, l % RING, :, :], bw_tok[:, :, :],
                                                    ALU.mult).then_inc(level_ready, 1)
                            pool.wait_ge(bwT_ready, n + 1)
                            pool.wait_ge(midT_ready, NL * n + l + 1)
                            nc.gpsimd.tensor_tensor(halves(mid_T(l), l, 0), halves(mid_T(l), l, 0),
                                                    halves(bwT[:, :, :], l, 0), ALU.mult).then_inc(left_ready, 1)
                        pool.wait_ge(end_ready, 3 * n + 2)
                        nc.gpsimd.tensor_tensor(decay_end[:, :, :], decay_end[:, :, :], bw_tok[:, 0:HG, :], ALU.mult
                                                ).then_inc(end_ready, 1)


def program(nc, io):
    with ExitStack() as ctx:
        c = Chip(nc, ctx, io)
        load_stage(c)
        norm_stage(c, "n1", True, False, io["L0_attn_ln1_w"], 1e-6)
        with ExitStack() as l0:
            gate_T = c.sb("gate_T", [P, NT * P], ctx=l0)
            per_token = c.sb("per_token", [P, 5, NG, B, U], ctx=l0)
            with ExitStack() as narrow:
                f_T = c.sb("f_T", [P, NT * P], ctx=narrow)
                narrow_stage(c, "n0", io["L0_attn_wfa"], io["L0_attn_wga"], io["L0_attn_wb"], f_T, gate_T,
                             per_token[:, 4])
                decay_stage(c, io["L0_attn_wfb"], io["L0_attn_dt_bias"], io["L0_attn_a_log"], f_T, per_token)
            delta_stage(c, io, gate_T, per_token)
        c.renew_sems()
        norm_stage(c, "n2", True, False, io["L0_attn_ln2_w"], 1e-6)
        dense_stage(c, "mlp", io["L0_attn_w_gate"], io["L0_attn_w_up"], io["L0_attn_w_down"])
        norm_stage(c, "n3", False, True, None, 1e-5)
        dense_stage(c, "q", io["L0_ffn_w_gate"], io["L0_ffn_w_up"], io["L0_ffn_w_down"],
                    (io["L0_ffn_s_gate"], io["L0_ffn_s_up"], io["L0_ffn_s_down"]))
        norm_stage(c, "n4", False, False, None, 1e-5)
        slots_stages(c, io)
        c.renew_sems()
        norm_stage(c, "n5", False, False, None, 1e-5)
        with ExitStack() as moe:
            gates_T = c.sb("gates_T", [NE + NS, NT * P], ctx=moe)
            route_stage(c, io, gates_T)
            experts_stage(c, io, gates_T)
        norm_stage(c, "n6", False, True, None, 1e-5, to_out=True)


def kernel(**inputs):
    import concourse.bacc as bacc
    from concourse.bass_utils import run_bass_kernel_spmd

    nc = bacc.Bacc("TRN2", target_bir_lowering=False, num_devices=1)
    arrays = {name: np.ascontiguousarray(a) for name, a in inputs.items()}
    arrays = {name: a.view(np.int32) if a.dtype == np.int8 else a for name, a in arrays.items()}
    arrays["squares"], arrays["expert_of_column"] = shape_constants()
    io = {name: nc.dram_tensor(name, a.shape, mybir.dt.from_np(a.dtype), kind="ExternalInput").ap()
          for name, a in arrays.items()}
    out = nc.dram_tensor("out", (B * T, D), F32, kind="ExternalOutput").ap()
    io["out"] = out.rearrange("(n p) d -> p n d", p=P)
    program(nc, io)
    result = run_bass_kernel_spmd(nc, [arrays], core_ids=[0])
    return result.results[0]["out"].reshape(B, T, D)
```
